# Optimizing a Trainium2 kernel written in Bass

```python
import numpy as np
import jax
import jax.numpy as jnp

def _softmax(x, axis=-1):
    return jax.nn.softmax(x, axis=axis)

def _gelu(x):
    return jax.nn.gelu(x, approximate=True)

def _silu(x):
    return jax.nn.silu(x)

def _sigmoid(x):
    return jax.nn.sigmoid(x)

def _layernorm(x, axis=-1, eps=1e-05):
    m = jnp.mean(x, axis=axis, keepdims=True)
    v = jnp.var(x, axis=axis, keepdims=True)
    return (x - m) / jnp.sqrt(v + eps)

def _scatter_add(tgt, idx, src, axis=0):
    return tgt.at[idx].add(src)

def _segment_sum(src, seg, n):
    return jax.ops.segment_sum(src, seg, n)
kernel_name = 'mk_adj_preln_d4_adj_r2_5ff1fe'

def setup_inputs(seed: int=0):
    np.random.seed(seed)
    _w = jnp.asarray

    def _rec_inputs():
        import jax
        import jax.numpy as jnp
        _gk = jax.random.key(seed)
        x = -0.000929 + 1 * jax.random.normal(jax.random.fold_in(_gk, 1), (4096, 128), jnp.float32)
        _a = jax.random.bernoulli(jax.random.fold_in(_gk, 2), 0.000976562, (4096, 4096))
        _a = jnp.logical_or(_a, jnp.swapaxes(_a, -1, -2))
        _a = jnp.logical_or(_a, jnp.eye(4096, dtype=bool))
        _af = _a.astype(jnp.float32)
        _af = _af * jax.random.uniform(jax.random.fold_in(_gk, 3), (4096, 4096), jnp.float32, 0.05, 1)
        adj = _af
        return (x, adj)
    x, adj = _rec_inputs()

    def _L0_gnn_setup():
        import jax, jax.numpy as jnp
        import numpy as np
        N, E, D = (4096, 4096, 128)
        key = jax.random.key(seed)
        k1, k2 = jax.random.split(key)
        X = jax.random.normal(k1, (N, D), dtype=jnp.float32)
        H = jax.random.uniform(k2, (N, E), dtype=jnp.float32)
        return {'X': X, 'H': H}
    _L0_gnn_all = _L0_gnn_setup()
    _L0_gnn_in = {k: v for k, v in _L0_gnn_all.items() if k in ()}
    del _L0_gnn_all

    def _L1_gnn_setup():
        import jax, jax.numpy as jnp
        import numpy as np
        N = 4096
        F = 128
        key = jax.random.key(seed)
        k1, k2, k3 = jax.random.split(key, 3)
        x = jax.random.normal(k1, (N, F), dtype=jnp.float32)
        adj = jax.random.uniform(k2, (N, N), dtype=jnp.float32)
        limit = float(np.sqrt(6.0 / (F + F)))
        weight = jax.random.uniform(k3, (F, F), dtype=jnp.float32, minval=-limit, maxval=limit)
        return {'x': x, 'adj': adj, 'weight': weight}
    _L1_gnn_all = _L1_gnn_setup()
    _L1_gnn_in = {k: v for k, v in _L1_gnn_all.items() if k in ('weight',)}
    del _L1_gnn_all

    def _L2_gnn_setup():
        import jax, jax.numpy as jnp
        import numpy as np
        N = 4096
        IN_DIM = 128
        OUT_DIM = 128
        EDGE_P = 0.002
        key = jax.random.key(seed)
        k1, k2, k3, k4 = jax.random.split(key, 4)
        H = jax.random.normal(k1, (N, IN_DIM), dtype=jnp.float32)
        A = (jax.random.uniform(k2, (N, N)) < EDGE_P).astype(jnp.float32)
        limit = np.sqrt(6.0 / (IN_DIM + OUT_DIM)).astype(np.float32)
        W = jax.random.uniform(k3, (OUT_DIM, IN_DIM), minval=-limit, maxval=limit, dtype=jnp.float32)
        bound = 1.0 / np.sqrt(IN_DIM)
        b = jax.random.uniform(k4, (OUT_DIM,), minval=-bound, maxval=bound, dtype=jnp.float32)
        return {'H': H, 'A': A, 'W': W, 'b': b}
    _L2_gnn_all = _L2_gnn_setup()
    _L2_gnn_in = {k: v for k, v in _L2_gnn_all.items() if k in ('W', 'b')}
    del _L2_gnn_all

    def _L3_gnn_setup():
        import jax, jax.numpy as jnp
        import numpy as np
        NEG_SLOPE = 0.01
        N_U, N_V = (4096, 4096)
        U_F, V_F = (128, 128)
        HIDS = [128, 128]
        NUM_ROUNDS = 3

        def _glorot(key, fan_in, fan_out):
            lim = np.sqrt(6.0 / (fan_in + fan_out)).astype(np.float32)
            return jax.random.uniform(key, (fan_in, fan_out), jnp.float32, -lim, lim)

        def _mlp(x, W1, b1, W2, b2, W3, b3):
            a = jax.nn.leaky_relu
            x = a(x @ W1 + b1, NEG_SLOPE)
            x = a(x @ W2 + b2, NEG_SLOPE)
            return a(x @ W3 + b3, NEG_SLOPE)
        key = jax.random.key(seed)
        ks = jax.random.split(key, 12)
        inp = {'u_node_feats': jax.random.normal(ks[0], (N_U, U_F), jnp.float32), 'v_node_feats': jax.random.normal(ks[1], (N_V, V_F), jnp.float32), 'uv_adj_mat': jax.random.uniform(ks[2], (N_V, N_U), jnp.float32), 'vu_adj_mat': jax.random.uniform(ks[3], (N_U, N_V), jnp.float32)}
        dims_uv = [U_F] + HIDS + [V_F]
        dims_vu = [V_F] + HIDS + [U_F]
        k = 4
        for tag, dims in (('uv', dims_uv), ('vu', dims_vu)):
            for i in range(3):
                inp[f'{tag}_W{i + 1}'] = _glorot(ks[k], dims[i], dims[i + 1])
                k += 1
                inp[f'{tag}_b{i + 1}'] = jnp.zeros((dims[i + 1],), jnp.float32)
        return inp
    _L3_gnn_all = _L3_gnn_setup()
    _L3_gnn_in = {k: v for k, v in _L3_gnn_all.items() if k in ('v_node_feats', 'uv_W1', 'uv_b1', 'uv_W2', 'uv_b2', 'uv_W3', 'uv_b3', 'vu_W1', 'vu_b1', 'vu_W2', 'vu_b2', 'vu_W3', 'vu_b3')}
    del _L3_gnn_all
    return {'x': x, 'adj': adj, 'L1_gnn_weight': _L1_gnn_in['weight'], 'L2_gnn_W': _L2_gnn_in['W'], 'L2_gnn_b': _L2_gnn_in['b'], 'L3_gnn_v_node_feats': _L3_gnn_in['v_node_feats'], 'L3_gnn_uv_W1': _L3_gnn_in['uv_W1'], 'L3_gnn_uv_b1': _L3_gnn_in['uv_b1'], 'L3_gnn_uv_W2': _L3_gnn_in['uv_W2'], 'L3_gnn_uv_b2': _L3_gnn_in['uv_b2'], 'L3_gnn_uv_W3': _L3_gnn_in['uv_W3'], 'L3_gnn_uv_b3': _L3_gnn_in['uv_b3'], 'L3_gnn_vu_W1': _L3_gnn_in['vu_W1'], 'L3_gnn_vu_b1': _L3_gnn_in['vu_b1'], 'L3_gnn_vu_W2': _L3_gnn_in['vu_W2'], 'L3_gnn_vu_b2': _L3_gnn_in['vu_b2'], 'L3_gnn_vu_W3': _L3_gnn_in['vu_W3'], 'L3_gnn_vu_b3': _L3_gnn_in['vu_b3']}

def reference(x, adj, L1_gnn_weight, L2_gnn_W, L2_gnn_b, L3_gnn_v_node_feats, L3_gnn_uv_W1, L3_gnn_uv_b1, L3_gnn_uv_W2, L3_gnn_uv_b2, L3_gnn_uv_W3, L3_gnn_uv_b3, L3_gnn_vu_W1, L3_gnn_vu_b1, L3_gnn_vu_W2, L3_gnn_vu_b2, L3_gnn_vu_W3, L3_gnn_vu_b3):
    import jax
    import jax.numpy as jnp

    def _L0_gnn_ref(X, H):
        import jax, jax.numpy as jnp
        import numpy as np
        N, E, D = (4096, 4096, 128)
        msg = jnp.matmul(H.T, X)
        inv_deg = 1.0 / H.sum(axis=0)
        inv_deg = jnp.where(jnp.isinf(inv_deg), 0.0, inv_deg)
        return msg * inv_deg[:, None]

    def _L1_gnn_ref(x, adj, weight):
        import jax, jax.numpy as jnp
        import numpy as np
        N = 4096
        F = 128
        n = adj.shape[0]
        adj_hat = adj + jnp.eye(n, dtype=adj.dtype)
        deg = jnp.sum(adj_hat, axis=1)
        d_inv_sqrt = (deg + 1e-08) ** (-0.5)
        support = d_inv_sqrt[:, None] * adj_hat * d_inv_sqrt[None, :]
        out = jnp.matmul(jnp.matmul(support, x), weight)
        return jax.nn.relu(out)

    def _L2_gnn_ref(H, A, W, b):
        import jax, jax.numpy as jnp
        import numpy as np
        N = 4096
        IN_DIM = 128
        OUT_DIM = 128
        EDGE_P = 0.002
        n = A.shape[0]
        A_t = A + jnp.eye(n, dtype=A.dtype)
        D = A_t.sum(axis=1)
        D_inv = jnp.where(D > 0, D ** (-0.5), jnp.zeros_like(D))
        A_norm = D_inv[:, None] * A_t * D_inv[None, :]
        HW = H @ W.T + b
        return jax.nn.relu(A_norm @ HW)

    def _L3_gnn_ref(u_node_feats, v_node_feats, uv_adj_mat, vu_adj_mat, uv_W1, uv_b1, uv_W2, uv_b2, uv_W3, uv_b3, vu_W1, vu_b1, vu_W2, vu_b2, vu_W3, vu_b3):
        import jax, jax.numpy as jnp
        import numpy as np
        NEG_SLOPE = 0.01
        N_U, N_V = (4096, 4096)
        U_F, V_F = (128, 128)
        HIDS = [128, 128]
        NUM_ROUNDS = 3

        def _glorot(key, fan_in, fan_out):
            lim = np.sqrt(6.0 / (fan_in + fan_out)).astype(np.float32)
            return jax.random.uniform(key, (fan_in, fan_out), jnp.float32, -lim, lim)

        def _mlp(x, W1, b1, W2, b2, W3, b3):
            a = jax.nn.leaky_relu
            x = a(x @ W1 + b1, NEG_SLOPE)
            x = a(x @ W2 + b2, NEG_SLOPE)
            return a(x @ W3 + b3, NEG_SLOPE)
        u, v = (u_node_feats, v_node_feats)
        for _ in range(NUM_ROUNDS):
            v = _mlp(uv_adj_mat @ u, uv_W1, uv_b1, uv_W2, uv_b2, uv_W3, uv_b3)
            u = _mlp(vu_adj_mat @ v, vu_W1, vu_b1, vu_W2, vu_b2, vu_W3, vu_b3)
        return v
    h = jnp.maximum(_layernorm(x, axis=-1), 0.0)
    x = x + _L0_gnn_ref(h, adj)
    h = jnp.maximum(_layernorm(x, axis=-1), 0.0)
    x = x + _L1_gnn_ref(h, adj, L1_gnn_weight)
    h = jnp.maximum(_layernorm(x, axis=-1), 0.0)
    x = x + _L2_gnn_ref(h, adj, L2_gnn_W, L2_gnn_b)
    h = jnp.maximum(_layernorm(x, axis=-1), 0.0)
    x = x + _L3_gnn_ref(h, L3_gnn_v_node_feats, adj, adj, L3_gnn_uv_W1, L3_gnn_uv_b1, L3_gnn_uv_W2, L3_gnn_uv_b2, L3_gnn_uv_W3, L3_gnn_uv_b3, L3_gnn_vu_W1, L3_gnn_vu_b1, L3_gnn_vu_W2, L3_gnn_vu_b2, L3_gnn_vu_W3, L3_gnn_vu_b3)
    return x

_drawn_inputs = setup_inputs


def setup_inputs(seed=0):
    import zlib

    import numpy as np

    out = dict(_drawn_inputs(seed))
    spreads = {'L3_gnn_uv_b1': (0.0, 0.399),
     'L3_gnn_uv_b2': (0.0, 0.359),
     'L3_gnn_uv_b3': (0.0, 0.1),
     'L3_gnn_vu_b1': (0.0, 0.577),
     'L3_gnn_vu_b2': (0.0, 0.596),
     'L3_gnn_vu_b3': (0.0, 0.388)}
    factors = {'L2_gnn_b': 3.1}
    for name, (base, spread) in spreads.items():
        noise = np.random.default_rng([zlib.crc32(name.encode()), seed]).standard_normal(out[name].shape)
        drawn = base * np.exp(spread * noise) if base else spread * noise
        out[name] = jnp.asarray(drawn.astype(out[name].dtype))
    for name, factor in factors.items():
        out[name] = (out[name] * factor).astype(out[name].dtype)
    return out
```

```python
from contextlib import ExitStack

import concourse.bass as bass
from concourse import mybir

F32 = mybir.dt.float32
F32R = mybir.dt.float32r
ALU = mybir.AluOpType
ACT = mybir.ActivationFunctionType
AX = mybir.AxisListType

P = 128
N = 4096
KT = N // P
BANK = 512
WIDE = 2 * BANK
SC = N // WIDE
TH = BANK // P
HALVES = KT // TH

KEPT = (7, 15, 23, 31)
STREAMED = tuple(k for k in range(KT) if k not in KEPT)
RING = 4
HI = 4
LO = 2
LN_EPS = 1e-5
SLOPE = 0.01
WEIGHT_LOADS = 3 + 2 * 6 + 2

MLP0 = 3
ROUNDS = 2


def build(nc, x, adj, adj_t, w_l1, w_l2t, b_l2, mlp_w, mlp_b, out):
    with ExitStack() as ctx:
        def sb(name, shape, dt=F32):
            return ctx.enter_context(nc.sbuf_tensor(name, shape, dt))

        def sem(name):
            return ctx.enter_context(nc.semaphore(name))

        def sems(name, n):
            return [sem(f"{name}{i}") for i in range(n)]

        kept = sb("kept", [P, SC * len(KEPT), WIDE])
        ring = sb("ring", [P, RING, WIDE])
        hi = sb("hi", [P, HI, WIDE], F32R)
        lo = sb("lo", [P, LO, WIDE], F32R)
        h_hi = [sb(f"h_hi{i}", [P, KT, P], F32R) for i in range(2)]
        h_lo = [sb(f"h_lo{i}", [P, KT, P], F32R) for i in range(2)]
        xs = sb("xs", [P, KT, P])
        cols = sb("cols", [P, 2, TH, P])
        temp = sb("temp", [P, 2, TH, P])
        rows = sb("rows", [P, 2, TH, P])
        wl1 = sb("wl1", [P, P])
        wl2 = sb("wl2", [P, P])
        bl2 = sb("bl2", [1, P])
        mw = sb("mw", [P, 6, P])
        mb = sb("mb", [P, 6])
        mb3 = sb("mb3", [1, 2, P])
        ident = sb("ident", [P, P])
        ident_r = sb("ident_r", [P, P], F32R)
        ones_r = sb("ones_r", [P, P], F32R)
        ones_f = sb("ones_f", [P, P])
        stats = sb("stats", [P, 2, TH, 6])
        mean_var = sb("mean_var", [P, 2, TH, 2])
        mean1 = sb("mean1", [P, KT])
        rstd1 = sb("rstd1", [P, KT])
        var_eps = sb("var_eps", [P, 2, TH])
        rstd = sb("rstd", [P, 2, TH])
        minus_half = sb("minus_half", [P, 2 * KT])
        col_sum = sb("col_sum", [P, 2, TH])
        inv_raw = sb("inv_raw", [P, 2, TH])
        inv_cap = sb("inv_cap", [P, 2, TH])
        inv_fin = sb("inv_fin", [P, 2, TH])
        inv_deg = sb("inv_deg", [P, 2, TH])
        row_part = sb("row_part", [P, KT, SC])
        row_sum = sb("row_sum", [P, KT])
        degree = sb("degree", [P, 2, KT])
        deg_pow = sb("deg_pow", [P, 2, KT])
        deg_pos = sb("deg_pos", [P, KT])
        d_inv1 = deg_pow[:, 0, :]
        d_inv2 = sb("d_inv2", [P, KT])
        scale1 = sb("scale1", [P, KT])

        ps = ctx.enter_context(nc.psum_tensor("ps", [P, 8 * BANK], F32))

        def acc(parity, h, a=0, b=BANK):
            return ps[:, bass.ds((parity * 2 + h) * BANK + a, b - a)]

        def csum(h):
            return ps[:, (4 + h) * BANK:(5 + h) * BANK]

        def tail(h, q=None):
            base = (6 + h) * BANK
            return ps[:, base:base + BANK] if q is None else ps[:, base + q * P:base + (q + 1) * P]

        x_landed = sems("x_landed", HALVES)
        w_landed = sem("w_landed")
        ident_zeroed = sem("ident_zeroed")
        ident_made = sem("ident_made")
        consts_made = sem("consts_made")
        consts_rounded = sem("consts_rounded")
        ring_landed = sems("ring_landed", RING)
        kept_landed = sems("kept_landed", len(KEPT))
        hi_ready = sem("hi_ready")
        lo_ready = sem("lo_ready")
        pieces_used = sem("pieces_used")
        h_ready = sem("h_ready")
        acc_copied = sem("acc_copied")
        csum_read = sem("csum_read")
        stats_done = sems("stats_done", 2)
        aggr_done = sems("aggr_done", 2)
        var_ready = sems("var_ready", 2)
        rstd_ready = sems("rstd_ready", 2)
        normed = sems("normed", 2)
        x_updated = sems("x_updated", 2)
        x_kept = sems("x_kept", 2)
        h_hi_ready = sems("h_hi_ready", 2)
        inv_step = sems("inv_step", 2)
        cols_copied = sems("cols_copied", 2)
        turned = sems("turned", 2)
        relu_ready = sems("relu_ready", 2)
        norm_turned = sems("norm_turned", 2)
        norm_t_copied = sems("norm_t_copied", 2)
        hw_done = sems("hw_done", 2)
        lin_done = [sems(f"lin{i}_done", 2) for i in range(3)]
        pre_ready = [sems(f"pre{i}_ready", 2) for i in range(3)]
        act_ready = [sems(f"act{i}_ready", 2) for i in range(3)]
        mean_kept = sem("mean_kept")
        deg_step = sem("deg_step")
        deg_ready = sem("deg_ready")
        deg_pow_ready = sem("deg_pow_ready")
        d_inv_ready = sem("d_inv_ready")
        out_ready = sems("out_ready", 2)
        out_stored = sems("out_stored", 2)

        PER = KT

        def occurrence(G):
            return HALVES // 2 + G

        def tile0(G, s, h):
            return s * (2 * TH) + h * TH

        def run(bulk, steps):
            for k in range(KT):
                if bulk is not None:
                    bulk(k)
                for step in steps.get(k, ()):
                    step()

        def slots(table, *args):
            steps = {}
            for a, b, f in table:
                for h, k in ((0, a), (1, b)):
                    steps.setdefault(k, []).append(lambda f=f, h=h: f(h, *args))
            return steps

        def whole_program(eng, superchunk, tails, boundary, last_tail, unrolled=False):
            superchunk(0, 0, 0, {})
            with eng.Fori(1, SC) as s:
                superchunk(s, 0, s, tails["message"](s - 1, s - 1))
            run(None, tails["message"](SC - 1, SC - 1))
            boundary()
            superchunk(SC, 1, 0, {})
            if unrolled:
                for s in range(1, SC):
                    superchunk(SC + s, 1, s, tails["conv1"](SC + s - 1, s - 1))
            else:
                with eng.Fori(1, SC) as s:
                    superchunk(SC + s, 1, s, tails["conv1"](SC + s - 1, s - 1))
            superchunk(2 * SC, 2, 0, tails["conv1"](2 * SC - 1, SC - 1))
            if unrolled:
                for s in range(1, SC):
                    superchunk(2 * SC + s, 2, s, tails["conv2"](2 * SC + s - 1, s - 1))
            else:
                with eng.Fori(1, SC) as s:
                    superchunk(2 * SC + s, 2, s, tails["conv2"](2 * SC + s - 1, s - 1))
            superchunk(3 * SC, 3, 0, tails["conv2"](3 * SC - 1, SC - 1))
            with eng.Fori(0, ROUNDS) as r:
                base = MLP0 * SC + r * (2 * SC)
                with eng.Fori(1, SC) as s:
                    superchunk(base + s, MLP0, s, tails["uv"](base + s - 1, s - 1))
                superchunk(base + SC, MLP0 + 1, 0, tails["uv"](base + SC - 1, SC - 1))
                with eng.Fori(1, SC) as s:
                    superchunk(base + SC + s, MLP0 + 1, s, tails["vu"](base + SC + s - 1, s - 1))
                superchunk(base + 2 * SC, MLP0 + 2, 0, tails["vu"](base + 2 * SC - 1, SC - 1))
            base = (MLP0 + 2 * ROUNDS) * SC
            with eng.Fori(1, SC) as s:
                superchunk(base + s, MLP0, s, tails["last"](base + s - 1, s - 1))
            run(None, tails["last"](base + SC - 1, SC - 1))
            last_tail()

        def mlp_turn(G):
            return G - MLP0 * SC

        def piece_source(k, s, G):
            if k in KEPT:
                return kept[:, bass.ds(s * len(KEPT) + KEPT.index(k), 1), :].rearrange("p a n -> p (a n)")
            return ring[:, STREAMED.index(k) % RING, :]

        block = ctx.enter_context(nc.Block())

        @block.sync
        def _(eng):
            eng.dma_start(wl1[:, :], w_l1).then_inc(w_landed, 16)
            eng.dma_start(wl2[:, :], w_l2t).then_inc(w_landed, 16)
            eng.dma_start(bl2[:, :], b_l2.rearrange("(a f) -> a f", a=1)).then_inc(w_landed, 16)
            for i in range(6):
                eng.dma_start(mw[:, i, :], mlp_w[i]).then_inc(w_landed, 16)
                eng.dma_start(mb[:, i:i + 1], mlp_b[i].rearrange("(f a) -> f a", a=1)).then_inc(w_landed, 16)
            for i in range(2):
                eng.dma_start(mb3[:, i, :], mlp_b[3 * i + 2].rearrange("(a f) -> a f", a=1)).then_inc(w_landed, 16)

            def superchunk(G, p, s, steps):
                src = adj if p == 0 else adj_t
                for k in range(KT):
                    piece = src[k * P:(k + 1) * P, bass.ds(s * WIDE, WIDE)]
                    if k in KEPT:
                        if p > 1:
                            continue
                        if p == 1:
                            eng.wait_ge(lo_ready, (G - SC) * PER + k + 1)
                        eng.dma_start(kept[:, bass.ds(s * len(KEPT) + KEPT.index(k), 1), :]
                                      .rearrange("p a n -> p (a n)"), piece)\
                           .then_inc(kept_landed[KEPT.index(k)], 16)
                        continue
                    m = STREAMED.index(k)
                    if m >= RING:
                        eng.wait_ge(lo_ready, G * PER + STREAMED[m - RING] + 1)
                    elif not (isinstance(G, int) and G == 0):
                        eng.wait_ge(lo_ready, (G - 1) * PER + STREAMED[len(STREAMED) + m - RING] + 1)
                    eng.dma_start(ring[:, m % RING, :], piece).then_inc(ring_landed[m % RING], 16)

            no_tails = dict.fromkeys(("message", "conv1", "conv2", "uv", "vu", "last"), lambda G, s: {})

            def stores_landed():
                for h in range(2):
                    eng.wait_ge(out_stored[h], 16 * SC)

            whole_program(eng, superchunk, no_tails, lambda: None, stores_landed)

        @block.scalar
        def _(eng):
            for j in range(HALVES):
                eng.dma_start(xs[:, j * TH:(j + 1) * TH, :],
                              x[j * BANK:(j + 1) * BANK, :].rearrange("(t p) f -> p t f", p=P))\
                   .then_inc(x_landed[j], 16)
            eng.wait_ge(ident_made, 1)
            eng.activation(ident_r[:, :], ident[:, :], ACT.Copy).then_inc(consts_rounded, 1)
            eng.wait_ge(consts_made, 1)
            eng.activation(ones_r[:, :], ones_f[:, :], ACT.Copy).then_inc(consts_rounded, 1)

            eng.wait_ge(w_landed, 16 * WEIGHT_LOADS)

            def round_rows(h, o, parity, t0, func):
                eng.wait_ge(normed[h], o + 1)
                eng.activation(h_hi[parity][:, bass.ds(t0, TH), :], rows[:, h, :, :], func)\
                   .then_inc(h_hi_ready[h], 1)

            for j in range(HALVES):
                round_rows(j % 2, j // 2, 0, j * TH, ACT.Relu)

            def superchunk(G, p, s, steps):
                def bulk(k):
                    n = G * PER + k
                    if k in KEPT:
                        if p <= 1:
                            eng.wait_ge(kept_landed[KEPT.index(k)], 16 * (G + 1))
                    else:
                        m = STREAMED.index(k)
                        eng.wait_ge(ring_landed[m % RING],
                                    16 * (G * (len(STREAMED) // RING) + m // RING + 1))
                    if not (isinstance(G, int) and n < HI):
                        eng.wait_ge(pieces_used, n - HI + 1)
                    if p == 0:
                        eng.activation(hi[:, k % HI, :], piece_source(k, s, G), ACT.Copy,
                                       accum_out=row_part[:, k, bass.ds(s, 1)]).then_inc(hi_ready, 1)
                    else:
                        eng.activation(hi[:, k % HI, :], piece_source(k, s, G), ACT.Copy)\
                           .then_inc(hi_ready, 1)
                run(bulk, steps)

            def copy_acc(h, G, s):
                eng.wait_ge(pieces_used, (G + 1) * PER)
                eng.activation(cols[:, h, :, :].rearrange("p q f -> p (q f)"), acc(s % 2, h), ACT.Copy)\
                   .then_inc(acc_copied, 1)

            def copy_norm(h, G, s):
                eng.wait_ge(norm_turned[h], G - SC + 1)
                eng.activation(cols[:, h, :, :].rearrange("p q f -> p (q f)"), tail(h), ACT.Relu)\
                   .then_inc(norm_t_copied[h], 1)

            def scale_hi(h, G, s):
                eng.wait_ge(hw_done[h], G - SC + 1)
                t0 = tile0(G, s, h)
                for q in range(TH):
                    op = eng.activation(h_hi[0][:, bass.ds(t0 + q, 1), :].rearrange("p a f -> p (a f)"),
                                        tail(h, q), ACT.Identity, scale=d_inv2[:, bass.ds(t0 + q, 1)])
                op.then_inc(h_hi_ready[h], 1)

            def norm_hi(h, G, s):
                round_rows(h, occurrence(G), 1, tile0(G, s, h), ACT.Relu)

            def biased(i, kind):
                def step(h, G, s):
                    eng.wait_ge(lin_done[i][h], mlp_turn(G) + 1)
                    to = temp[:, h, :, :].rearrange("p q f -> p (q f)")
                    if i < 2:
                        b = 3 * kind + i
                        eng.activation(to, tail(h), ACT.Identity, bias=mb[:, b:b + 1])\
                           .then_inc(pre_ready[i][h], 1)
                    else:
                        eng.activation(to, tail(h), ACT.Copy).then_inc(pre_ready[i][h], 1)
                return step

            def mlp_hi(kind):
                def step(h, G, s):
                    eng.wait_ge(act_ready[2][h], mlp_turn(G) + 1)
                    eng.activation(h_hi[kind][:, bass.ds(tile0(G, s, h), TH), :], rows[:, h, :, :], ACT.Copy)\
                       .then_inc(h_hi_ready[h], 1)
                return step

            def store_out(h, G, s):
                turn = G - (MLP0 + 2 * ROUNDS) * SC + 1
                eng.wait_ge(out_ready[h], turn)
                eng.dma_start(out[bass.ds(s * WIDE + h * BANK, BANK), :].rearrange("(t p) f -> p t f", p=P),
                              xs[:, bass.ds(tile0(G, s, h), TH), :]).then_inc(out_stored[h], 16)

            def mlp(kind):
                return lambda G, s: slots([(3, 4, copy_acc), (6, 7, biased(0, kind)), (9, 10, biased(1, kind)),
                                           (12, 13, biased(2, kind)), (14, 15, mlp_hi(kind))], G, s)

            tails = {
                "message": lambda G, s: slots([(3, 4, copy_acc)], G, s),
                "conv1": lambda G, s: slots([(3, 4, copy_acc), (12, 14, copy_norm), (15, 17, scale_hi)], G, s),
                "conv2": lambda G, s: slots([(3, 4, copy_acc), (11, 13, norm_hi)], G, s),
                "uv": mlp(0),
                "vu": mlp(1),
                "last": lambda G, s: slots([(3, 4, copy_acc), (6, 7, biased(0, 0)), (9, 10, biased(1, 0)),
                                            (12, 13, biased(2, 0)), (16, 17, store_out)], G, s),
            }

            def boundary():
                for j in range(HALVES):
                    round_rows(j % 2, HALVES // 2 + j // 2, 1, j * TH, ACT.Relu)

            whole_program(eng, superchunk, tails, boundary, lambda: None)

        @block.vector
        def _(eng):
            eng.memset(ones_f[:, :], 1.0).then_inc(consts_made, 1)
            eng.memset(minus_half[:, :], -0.5).then_inc(consts_made, 1)

            def norm_stats(h, o, src, keep=None):
                for q in range(TH):
                    op = eng.bn_stats(stats[:, h, q, :], src[:, q, :])
                op.then_inc(stats_done[h], 1)
                eng.wait_ge(stats_done[h], o + 1)
                if keep is not None:
                    keep()
                for q in range(TH):
                    op = eng.bn_aggr(mean_var[:, h, q, :], stats[:, h, q, :])
                op.then_inc(aggr_done[h], 1)
                if not (isinstance(o, int) and o == 0):
                    eng.wait_ge(rstd_ready[h], o)
                eng.wait_ge(aggr_done[h], o + 1)
                eng.tensor_scalar(var_eps[:, h, :], mean_var[:, h, :, 1], LN_EPS, None, ALU.add)\
                   .then_inc(var_ready[h], 1)

            def norm_rows(h, src, mean, scale):
                for q in range(TH):
                    op = eng.tensor_scalar(rows[:, h, q, :], src[:, q, :], mean[:, q:q + 1], scale[:, q:q + 1],
                                           ALU.subtract, ALU.mult)
                op.then_inc(normed[h], 1)

            def low_rows(h, hi_count, parity, t0, op0):
                eng.wait_ge(h_hi_ready[h], hi_count + 1)
                eng.scalar_tensor_tensor(out=h_lo[parity][:, bass.ds(t0, TH), :], in0=rows[:, h, :, :],
                                         scalar=0.0 if op0 == ALU.max else 1.0,
                                         in1=h_hi[parity][:, bass.ds(t0, TH), :].bitcast(F32),
                                         op0=op0, op1=ALU.subtract).then_inc(h_ready, 1)

            for j in range(HALVES):
                h = j % 2
                eng.wait_ge(x_landed[j], 16)
                norm_stats(h, j // 2, xs[:, j * TH:(j + 1) * TH, :])
                eng.wait_ge(rstd_ready[h], j // 2 + 1)
                if j >= 2:
                    eng.wait_ge(h_ready, j - 1)
                norm_rows(h, xs[:, j * TH:(j + 1) * TH, :], mean_var[:, h, :, 0], rstd[:, h, :])
                low_rows(h, j // 2, 0, j * TH, ALU.max)

            def superchunk(G, p, s, steps):
                def bulk(k):
                    n = G * PER + k
                    eng.wait_ge(hi_ready, n + 1)
                    if not (isinstance(G, int) and n < LO):
                        eng.wait_ge(pieces_used, n - LO + 1)
                    eng.tensor_tensor(lo[:, k % LO, :], piece_source(k, s, G), hi[:, k % HI, :].bitcast(F32),
                                      ALU.subtract).then_inc(lo_ready, 1)
                run(bulk, steps)

            def take_col_sums(h, G, s):
                eng.wait_ge(pieces_used, (G + 1) * PER)
                if not (isinstance(G, int) and G == 0):
                    eng.wait_ge(x_updated[h], G)
                for q in range(TH):
                    op = eng.scalar_tensor_tensor(out=temp[:, h, q, :], in0=csum(h)[:, q * P:(q + 1) * P],
                                                  scalar=1.0, in1=ident[:, :], op0=ALU.mult, op1=ALU.mult,
                                                  accum_out=col_sum[:, h, q:q + 1])
                op.then_inc(csum_read, 1)

            def invert_col_sums(h, G, s):
                eng.wait_ge(csum_read, 2 * G + h + 1)
                eng.reciprocal(inv_raw[:, h, :], col_sum[:, h, :]).then_inc(inv_step[h], 1)
                eng.wait_ge(inv_step[h], 4 * G + 1)
                eng.tensor_scalar(inv_cap[:, h, :], inv_raw[:, h, :], 3.4028234e38, -3.4028234e38,
                                  ALU.min, ALU.max).then_inc(inv_step[h], 1)
                eng.wait_ge(inv_step[h], 4 * G + 2)
                eng.tensor_tensor(inv_fin[:, h, :], inv_raw[:, h, :], inv_cap[:, h, :], ALU.is_equal)\
                   .then_inc(inv_step[h], 1)
                eng.wait_ge(inv_step[h], 4 * G + 3)
                eng.tensor_tensor(inv_deg[:, h, :], inv_fin[:, h, :], inv_cap[:, h, :], ALU.mult)\
                   .then_inc(inv_step[h], 1)

            def keep_x(h, t0):
                eng.tensor_scalar(xs[:, bass.ds(t0, TH), :], rows[:, h, :, :], 1.0, None, ALU.mult)\
                   .then_inc(x_kept[h], 1)

            def add_message(h, G, s):
                eng.wait_ge(turned[h], G + 1)
                eng.wait_ge(inv_step[h], 4 * G + 4)
                t0 = tile0(G, s, h)
                for q in range(TH):
                    xt = xs[:, bass.ds(t0 + q, 1), :].rearrange("p a f -> p (a f)")
                    op = eng.scalar_tensor_tensor(out=rows[:, h, q, :], in0=tail(h, q),
                                                  scalar=inv_deg[:, h, q:q + 1],
                                                  in1=xt, op0=ALU.mult, op1=ALU.add)
                op.then_inc(x_updated[h], 1)
                eng.wait_ge(x_updated[h], G + 1)
                norm_stats(h, occurrence(G), rows[:, h, :, :], lambda: keep_x(h, t0))
                eng.tensor_copy(mean1[:, bass.ds(t0, TH)], mean_var[:, h, :, 0]).then_inc(mean_kept, 1)

            def boundary():
                eng.tensor_reduce(row_sum[:, :], row_part[:, :, :], AX.X, ALU.add).then_inc(deg_step, 1)
                eng.wait_ge(deg_step, 1)
                eng.tensor_scalar(degree[:, 0, :], row_sum[:, :], 1.0, 1e-8, ALU.add, ALU.add)\
                   .then_inc(deg_ready, 1)
                eng.tensor_scalar(degree[:, 1, :], row_sum[:, :], 1.0, 1.2e-38, ALU.add, ALU.max)\
                   .then_inc(deg_ready, 1)
                eng.tensor_scalar(deg_pos[:, :], row_sum[:, :], 1.0, 0.0, ALU.add, ALU.is_gt)\
                   .then_inc(deg_step, 1)
                eng.wait_ge(deg_step, 2)
                eng.wait_ge(deg_pow_ready, 1)
                eng.tensor_tensor(d_inv2[:, :], deg_pow[:, 1, :], deg_pos[:, :], ALU.mult)\
                   .then_inc(d_inv_ready, 1)
                for h in range(2):
                    eng.wait_ge(rstd_ready[h], HALVES // 2 + SC)
                eng.tensor_tensor(scale1[:, :], rstd1[:, :], d_inv1, ALU.mult).then_inc(d_inv_ready, 1)
                eng.wait_ge(d_inv_ready, 2)
                eng.wait_ge(mean_kept, HALVES)
                for j in range(HALVES):
                    h = j % 2
                    eng.wait_ge(h_ready, HALVES + j - 1)
                    a, b = j * TH, (j + 1) * TH
                    norm_rows(h, xs[:, a:b, :], mean1[:, a:b], scale1[:, a:b])
                    low_rows(h, HALVES // 2 + j // 2, 1, j * TH, ALU.max)

            def add_conv(scale):
                def step(h, G, s):
                    eng.wait_ge(turned[h], G + 1)
                    t0 = tile0(G, s, h)
                    for q in range(TH):
                        op = eng.tensor_scalar(temp[:, h, q, :], tail(h, q), scale[:, bass.ds(t0 + q, 1)], 0.0,
                                               ALU.mult, ALU.max)
                    op.then_inc(relu_ready[h], 1)
                    eng.wait_ge(relu_ready[h], G - SC + 1)
                    eng.tensor_tensor(rows[:, h, :, :], temp[:, h, :, :], xs[:, bass.ds(t0, TH), :], ALU.add)\
                       .then_inc(x_updated[h], 1)
                return step

            def stats_after(h, G, s):
                eng.wait_ge(x_updated[h], G + 1)
                norm_stats(h, occurrence(G), rows[:, h, :, :], lambda: keep_x(h, tile0(G, s, h)))

            def norm_after(h, G, s):
                eng.wait_ge(rstd_ready[h], occurrence(G) + 1)
                eng.wait_ge(x_kept[h], G + 1)
                norm_rows(h, rows[:, h, :, :], mean_var[:, h, :, 0], rstd[:, h, :])

            def scaled_low(h, G, s):
                eng.wait_ge(h_hi_ready[h], occurrence(G) + 1)
                t0 = tile0(G, s, h)
                for q in range(TH):
                    op = eng.scalar_tensor_tensor(
                        out=h_lo[0][:, bass.ds(t0 + q, 1), :].rearrange("p a f -> p (a f)"), in0=tail(h, q),
                        scalar=d_inv2[:, bass.ds(t0 + q, 1)],
                        in1=h_hi[0][:, bass.ds(t0 + q, 1), :].rearrange("p a f -> p (a f)").bitcast(F32),
                        op0=ALU.mult, op1=ALU.subtract)
                op.then_inc(h_ready, 1)

            def norm_low(h, G, s):
                low_rows(h, occurrence(G), 1, tile0(G, s, h), ALU.max)

            def leaky(i):
                def step(h, G, s):
                    eng.wait_ge(pre_ready[i][h], mlp_turn(G) + 1)
                    v = temp[:, h, :, :]
                    eng.scalar_tensor_tensor(out=rows[:, h, :, :], in0=v, scalar=SLOPE, in1=v,
                                             op0=ALU.mult, op1=ALU.max).then_inc(act_ready[i][h], 1)
                return step

            def mlp_low(kind):
                return lambda h, G, s: low_rows(h, occurrence(G), kind, tile0(G, s, h), ALU.mult)

            def add_out(h, G, s):
                eng.wait_ge(act_ready[2][h], mlp_turn(G) + 1)
                xt = xs[:, bass.ds(tile0(G, s, h), TH), :]
                eng.tensor_tensor(xt, xt, rows[:, h, :, :], ALU.add).then_inc(out_ready[h], 1)

            def mlp(kind):
                return lambda G, s: slots([(5, 6, leaky(0)), (8, 9, leaky(1)), (11, 12, leaky(2)),
                                           (13, 14, mlp_low(kind))], G, s)

            tails = {
                "message": lambda G, s: slots([(1, 1, take_col_sums), (2, 3, invert_col_sums), (4, 6, add_message)], G, s),
                "conv1": lambda G, s: slots([(4, 6, add_conv(d_inv1)), (5, 7, stats_after), (8, 10, norm_after),
                                             (13, 15, scaled_low)], G, s),
                "conv2": lambda G, s: slots([(4, 6, add_conv(d_inv2)), (5, 7, stats_after), (8, 10, norm_after),
                                             (11, 13, norm_low)], G, s),
                "uv": mlp(0),
                "vu": mlp(1),
                "last": lambda G, s: slots([(5, 6, leaky(0)), (8, 9, leaky(1)), (11, 12, leaky(2)),
                                            (13, 14, add_out)], G, s),
            }
            whole_program(eng, superchunk, tails, boundary, lambda: None)

        @block.gpsimd
        def _(eng):
            eng.memset(ident[:, :], 0.0).then_inc(ident_zeroed, 1)
            eng.wait_ge(ident_zeroed, 1)
            eng.affine_select(out=ident[:, :], in_=ident[:, :], compare_op=ALU.not_equal, fill=1.0,
                              base=0, pattern=[[-1, P]], channel_multiplier=1).then_inc(ident_made, 1)
            eng.wait_ge(consts_made, 2)

            def inv_root(h, o, to):
                eng.wait_ge(var_ready[h], o + 1)
                eng.tensor_tensor(to, var_eps[:, h, :], minus_half[:, 0:TH], ALU.pow)\
                   .then_inc(rstd_ready[h], 1)

            for j in range(HALVES):
                if j >= 2:
                    eng.wait_ge(normed[j % 2], j // 2)
                inv_root(j % 2, j // 2, rstd[:, j % 2, :])

            with eng.Fori(0, SC) as s:
                for h in range(2):
                    inv_root(h, occurrence(s), rstd1[:, bass.ds(tile0(s, s, h), TH)])
            eng.wait_ge(deg_ready, 2)
            eng.tensor_tensor(deg_pow[:, :, :].rearrange("p a t -> p (a t)"),
                              degree[:, :, :].rearrange("p a t -> p (a t)"), minus_half[:, :], ALU.pow)\
               .then_inc(deg_pow_ready, 1)
            with eng.Fori(SC, 3 * SC) as G:
                for h in range(2):
                    inv_root(h, occurrence(G), rstd[:, h, :])

        @block.tensor
        def _(eng):
            eng.wait_ge(consts_rounded, 2)
            eng.wait_ge(w_landed, 16 * WEIGHT_LOADS)

            def superchunk(G, p, s, steps):
                a, b = h_hi[p % 2], h_lo[p % 2]

                def bulk(k):
                    n = G * PER + k
                    first, last = k == 0, k == KT - 1
                    if isinstance(s, int) and s == 0 and k % TH == 0:
                        eng.wait_ge(h_ready, (G // SC) * HALVES + k // TH + 1 if isinstance(G, int)
                                    else G * 2 + (k // TH + 1))
                    if k == 0 and not (isinstance(G, int) and G < 2):
                        eng.wait_ge(acc_copied, 2 * (G - 1))
                    eng.wait_ge(hi_ready, n + 1)
                    for h in range(2):
                        eng.matmul(acc(s % 2, h), b[:, k, :], hi[:, k % HI, h * BANK:(h + 1) * BANK],
                                   start=first, stop=False)
                    for h in range(2):
                        eng.matmul(acc(s % 2, h), a[:, k, :], hi[:, k % HI, h * BANK:(h + 1) * BANK],
                                   start=False, stop=False)
                    if p in (1, 2) and k // (2 * TH) == s:
                        c = (k % TH) * P
                        for w in (b, a):
                            eng.matmul(acc(s % 2, k // TH % 2, c, c + P), w[:, k, :], ident_r[:, :],
                                       start=False, stop=False)
                    eng.wait_ge(lo_ready, n + 1)
                    for h in range(2):
                        op = eng.matmul(acc(s % 2, h), a[:, k, :], lo[:, k % LO, h * BANK:(h + 1) * BANK],
                                        start=False, stop=last)
                    if p == 0:
                        if k == 0 and not (isinstance(G, int) and G == 0):
                            eng.wait_ge(csum_read, 2 * G)
                        for h in range(2):
                            eng.matmul(csum(h), ones_r[:, :], hi[:, k % HI, h * BANK:(h + 1) * BANK],
                                       start=first, stop=False)
                        for h in range(2):
                            op = eng.matmul(csum(h), ones_r[:, :], lo[:, k % LO, h * BANK:(h + 1) * BANK],
                                            start=False, stop=last)
                    op.then_inc(pieces_used, 1)
                run(bulk, steps)

            def turn(h, G, s):
                eng.wait_ge(acc_copied, 2 * G + h + 1)
                for q in range(TH):
                    op = eng.transpose(tail(h, q), cols[:, h, q, :], ident[:, :])
                op.then_inc(turned[h], 1)

            def weigh(h, G, s):
                eng.wait_ge(acc_copied, 2 * G + h + 1)
                for q in range(TH):
                    op = eng.matmul(tail(h, q), cols[:, h, q, :], wl1[:, :], start=True, stop=True)
                op.then_inc(turned[h], 1)

            def turn_norm(h, G, s):
                eng.wait_ge(normed[h], occurrence(G) + 1)
                for q in range(TH):
                    op = eng.transpose(tail(h, q), rows[:, h, q, :], ident[:, :])
                op.then_inc(norm_turned[h], 1)

            def linear_rows(h, w, bias, lhs):
                for q in range(TH):
                    eng.matmul(tail(h, q), lhs[:, h, q, :], w, start=True, stop=False)
                    op = eng.matmul(tail(h, q), ones_f[0:1, :], bias, start=False, stop=True)
                return op

            def second_weight(h, G, s):
                eng.wait_ge(norm_t_copied[h], G - SC + 1)
                linear_rows(h, wl2[:, :], bl2[:, :], cols).then_inc(hw_done[h], 1)

            def layer(i, kind):
                def step(h, G, s):
                    if i == 0:
                        eng.wait_ge(acc_copied, 2 * G + h + 1)
                    else:
                        eng.wait_ge(act_ready[i - 1][h], mlp_turn(G) + 1)
                    w = mw[:, 3 * kind + i, :]
                    if i < 2:
                        src = cols if i == 0 else rows
                        eng.matmul(tail(h), w, src[:, h, :, :].rearrange("p q f -> p (q f)"),
                                   start=True, stop=True).then_inc(lin_done[i][h], 1)
                    else:
                        linear_rows(h, w, mb3[:, kind, :], rows).then_inc(lin_done[i][h], 1)
                return step

            def mlp(kind):
                return lambda G, s: slots([(1, 2, layer(0, kind)), (4, 5, layer(1, kind)),
                                           (7, 8, layer(2, kind))], G, s)

            tails = {
                "message": lambda G, s: slots([(1, 2, turn)], G, s),
                "conv1": lambda G, s: slots([(1, 2, weigh), (7, 9, turn_norm), (9, 11, second_weight)], G, s),
                "conv2": lambda G, s: slots([(1, 2, turn)], G, s),
                "uv": mlp(0),
                "vu": mlp(1),
                "last": mlp(0),
            }
            whole_program(eng, superchunk, tails, lambda: None, lambda: None, unrolled=True)


_INS = ["x", "adj", "L1_gnn_weight", "L2_gnn_W", "L2_gnn_b"] + [
    f"L3_gnn_{d}_{n}{i}" for d in ("uv", "vu") for n in ("W", "b") for i in (1, 2, 3)]


def kernel(**inputs):
    import numpy as np
    import concourse.bacc as bacc
    from concourse.bass_utils import run_bass_kernel_spmd

    arrays = {name: np.ascontiguousarray(inputs[name]) for name in _INS}
    arrays["adj_t"] = np.ascontiguousarray(np.asarray(inputs["adj"]).T)
    arrays["L2_gnn_W"] = np.ascontiguousarray(np.asarray(inputs["L2_gnn_W"]).T)

    nc = bacc.Bacc("TRN2", target_bir_lowering=False, num_devices=1)
    ap = {name: nc.dram_tensor(f"in_{name}", a.shape, mybir.dt.from_np(a.dtype), kind="ExternalInput").ap()
          for name, a in arrays.items()}
    out = nc.dram_tensor("out_0", (N, P), F32, kind="ExternalOutput").ap()
    build(nc, ap["x"], ap["adj"], ap["adj_t"], ap["L1_gnn_weight"], ap["L2_gnn_W"], ap["L2_gnn_b"],
          [ap[f"L3_gnn_{d}_W{i}"] for d in ("uv", "vu") for i in (1, 2, 3)],
          [ap[f"L3_gnn_{d}_b{i}"] for d in ("uv", "vu") for i in (1, 2, 3)], out)
    result = run_bass_kernel_spmd(nc, [{f"in_{name}": a for name, a in arrays.items()}], core_ids=[0])
    return result.results[0]["out_0"]
```

```python
from contextlib import ExitStack

import concourse.bass as bass
from concourse import mybir

F32 = mybir.dt.float32
F32R = mybir.dt.float32r
ALU = mybir.AluOpType
ACT = mybir.ActivationFunctionType
AX = mybir.AxisListType

P = 128
N = 4096
KT = N // P
BANK = 512
WIDE = 2 * BANK
SC = N // WIDE
TH = BANK // P
HALVES = KT // TH

KEPT = (7, 15, 23, 31)
STREAMED = tuple(k for k in range(KT) if k not in KEPT)
RING = 7
HI = 4
LO = 4
LN_EPS = 1e-5
SLOPE = 0.01
WEIGHT_LOADS = 3 + 2 * 6 + 2

MLP0 = 3
ROUNDS = 2


def build(nc, x, adj, adj_t, w_l1, w_l2t, b_l2, mlp_w, mlp_b, out):
    with ExitStack() as ctx:
        def sb(name, shape, dt=F32):
            return ctx.enter_context(nc.sbuf_tensor(name, shape, dt))

        def sem(name):
            return ctx.enter_context(nc.semaphore(name))

        def sems(name, n):
            return [sem(f"{name}{i}") for i in range(n)]

        kept = sb("kept", [P, SC * len(KEPT), WIDE])
        ring = sb("ring", [P, RING, WIDE])
        hi = sb("hi", [P, HI, WIDE], F32R)
        lo = sb("lo", [P, LO, WIDE], F32R)
        h_hi = sb("h_hi", [P, KT, P], F32R)
        h_lo = sb("h_lo", [P, KT, P], F32R)
        h_next = sb("h_next", [P, KT - 2 * TH, P])
        xs = sb("xs", [P, KT, P])
        cols = sb("cols", [P, 2, TH, P])
        rows = sb("rows", [P, 2, TH, P])
        wl1 = sb("wl1", [P, P])
        wl2 = sb("wl2", [P, P])
        bl2 = sb("bl2", [1, P])
        mw = sb("mw", [P, 6, P])
        mb = sb("mb", [P, 6])
        mb3 = sb("mb3", [1, 2, P])
        ident = sb("ident", [P, P])
        ident_r = sb("ident_r", [P, P], F32R)
        ones_r = sb("ones_r", [P, P], F32R)
        ones_f = sb("ones_f", [P, P])
        stats = sb("stats", [P, 2, TH, 6])
        mean_var = sb("mean_var", [P, 2, TH, 2])
        mean1 = sb("mean1", [P, KT])
        rstd1 = sb("rstd1", [P, KT])
        var_eps = sb("var_eps", [P, 2, TH])
        rstd = sb("rstd", [P, 2, TH])
        minus_half = sb("minus_half", [P, 2 * KT])
        col_sum = sb("col_sum", [P, 2, TH])
        inv_raw = sb("inv_raw", [P, 2, TH])
        inv_cap = sb("inv_cap", [P, 2, TH])
        inv_fin = sb("inv_fin", [P, 2, TH])
        inv_deg = sb("inv_deg", [P, 2, TH])
        row_part = sb("row_part", [P, KT, SC])
        row_sum = sb("row_sum", [P, KT])
        degree = sb("degree", [P, 2, KT])
        deg_pow = sb("deg_pow", [P, 2, KT])
        deg_pos = sb("deg_pos", [P, KT])
        d_inv1 = deg_pow[:, 0, :]
        d_inv2 = sb("d_inv2", [P, KT])
        scale1 = sb("scale1", [P, KT])

        ps = ctx.enter_context(nc.psum_tensor("ps", [P, 8 * BANK], F32))

        def acc(parity, h, a=0, b=BANK):
            return ps[:, bass.ds((parity * 2 + h) * BANK + a, b - a)]

        def csum(h):
            return ps[:, (4 + h) * BANK:(5 + h) * BANK]

        def tail(h, q=None):
            base = (6 + h) * BANK
            return ps[:, base:base + BANK] if q is None else ps[:, base + q * P:base + (q + 1) * P]

        x_landed = sems("x_landed", HALVES)
        w_landed = sem("w_landed")
        ident_zeroed = sem("ident_zeroed")
        ident_made = sem("ident_made")
        consts_made = sem("consts_made")
        consts_rounded = sem("consts_rounded")
        ring_landed = sems("ring_landed", RING)
        kept_landed = sems("kept_landed", len(KEPT))
        hi_ready = sem("hi_ready")
        lo_ready = sem("lo_ready")
        pieces_used = sem("pieces_used")
        h_hi_ready = sem("h_hi_ready")
        h_ready = sem("h_ready")
        acc_copied = sem("acc_copied")
        csum_read = sem("csum_read")
        stats_done = sems("stats_done", 2)
        aggr_done = sems("aggr_done", 2)
        var_ready = sems("var_ready", 2)
        rstd_ready = sems("rstd_ready", 2)
        normed = sems("normed", 2)
        x_updated = sems("x_updated", 2)
        x_kept = sems("x_kept", 2)
        inv_step = sems("inv_step", 2)
        cols_copied = sems("cols_copied", 2)
        turned = sems("turned", 2)
        relu_ready = sems("relu_ready", 2)
        norm_turned = sems("norm_turned", 2)
        norm_t_copied = sems("norm_t_copied", 2)
        hw_done = sems("hw_done", 2)
        scaled = sems("scaled", 2)
        lin_done = [sems(f"lin{i}_done", 2) for i in range(3)]
        pre_ready = [sems(f"pre{i}_ready", 2) for i in range(3)]
        act_ready = [sems(f"act{i}_ready", 2) for i in range(3)]
        mean_kept = sem("mean_kept")
        deg_step = sem("deg_step")
        deg_ready = sem("deg_ready")
        deg_pow_ready = sem("deg_pow_ready")
        d_inv_ready = sem("d_inv_ready")
        out_ready = sems("out_ready", 2)
        out_stored = sems("out_stored", 2)

        PER = KT

        def occurrence(G):
            return HALVES // 2 + G

        def tile0(G, s, h):
            return s * (2 * TH) + h * TH

        def run(bulk, steps):
            for k in range(KT):
                if bulk is not None:
                    bulk(k)
                for step in steps.get(k, ()):
                    step()

        def slots(table, *args):
            steps = {}
            for a, b, f in table:
                for h, k in ((0, a), (1, b)):
                    steps.setdefault(k, []).append(lambda f=f, h=h: f(h, *args))
            return steps

        def joined(first, second):
            return {k: first.get(k, []) + second.get(k, []) for k in first.keys() | second.keys()}

        def whole_program(eng, superchunk, tails, refill, boundary, last_tail, unrolled=False):
            def rest(base, p, kind):
                if unrolled and p in (1, 2):
                    for s in range(1, SC):
                        superchunk(base + s, p, s, tails[kind](base + s - 1, s - 1))
                    return
                if refill is None or kind == "message":
                    with eng.Fori(1, SC) as s:
                        superchunk(base + s, p, s, tails[kind](base + s - 1, s - 1))
                    return
                with eng.Fori(1, SC - 1) as s:
                    superchunk(base + s, p, s, tails[kind](base + s - 1, s - 1))
                superchunk(base + SC - 1, p, SC - 1,
                           joined(tails[kind](base + SC - 2, SC - 2), refill[kind](base)))

            superchunk(0, 0, 0, tails["start0"])
            rest(0, 0, "message")
            run(None, tails["message"](SC - 1, SC - 1))
            boundary()
            superchunk(SC, 1, 0, tails["start1"])
            rest(SC, 1, "conv1")
            superchunk(2 * SC, 2, 0, tails["conv1_end"](2 * SC - 1, SC - 1))
            rest(2 * SC, 2, "conv2")
            superchunk(3 * SC, 3, 0, tails["conv2_end"](3 * SC - 1, SC - 1))
            with eng.Fori(0, ROUNDS) as r:
                base = MLP0 * SC + r * (2 * SC)
                rest(base, 3, "uv")
                superchunk(base + SC, 4, 0, tails["uv_end"](base + SC - 1, SC - 1))
                rest(base + SC, 4, "vu")
                superchunk(base + 2 * SC, 5, 0, tails["vu_end"](base + 2 * SC - 1, SC - 1))
            base = (MLP0 + 2 * ROUNDS) * SC
            with eng.Fori(1, SC) as s:
                superchunk(base + s, 7, s, tails["last"](base + s - 1, s - 1))
            run(None, tails["last"](base + SC - 1, SC - 1))
            last_tail()

        def operand_count(G):
            return 2 * G

        def mlp_turn(G):
            return G - MLP0 * SC

        def piece_source(k, s, G):
            if k in KEPT:
                return kept[:, bass.ds(s * len(KEPT) + KEPT.index(k), 1), :].rearrange("p a n -> p (a n)")
            return ring[:, STREAMED.index(k) % RING, :]

        block = ctx.enter_context(nc.Block())

        @block.sync
        def _(eng):
            eng.dma_start(wl1[:, :], w_l1).then_inc(w_landed, 16)
            eng.dma_start(wl2[:, :], w_l2t).then_inc(w_landed, 16)
            eng.dma_start(bl2[:, :], b_l2.rearrange("(a f) -> a f", a=1)).then_inc(w_landed, 16)
            for i in range(6):
                eng.dma_start(mw[:, i, :], mlp_w[i]).then_inc(w_landed, 16)
                eng.dma_start(mb[:, i:i + 1], mlp_b[i].rearrange("(f a) -> f a", a=1)).then_inc(w_landed, 16)
            for i in range(2):
                eng.dma_start(mb3[:, i, :], mlp_b[3 * i + 2].rearrange("(a f) -> a f", a=1)).then_inc(w_landed, 16)

            def superchunk(G, p, s, steps):
                src = adj if p == 0 else adj_t
                for k in range(KT):
                    piece = src[k * P:(k + 1) * P, bass.ds(s * WIDE, WIDE)]
                    if k in KEPT:
                        if p > 1:
                            continue
                        if p == 1:
                            eng.wait_ge(lo_ready, (G - SC) * PER + k + 1)
                        eng.dma_start(kept[:, bass.ds(s * len(KEPT) + KEPT.index(k), 1), :]
                                      .rearrange("p a n -> p (a n)"), piece)\
                           .then_inc(kept_landed[KEPT.index(k)], 16)
                        continue
                    m = STREAMED.index(k)
                    if m >= RING:
                        eng.wait_ge(lo_ready, G * PER + STREAMED[m - RING] + 1)
                    elif not (isinstance(G, int) and G == 0):
                        eng.wait_ge(lo_ready, (G - 1) * PER + STREAMED[len(STREAMED) + m - RING] + 1)
                    eng.dma_start(ring[:, m % RING, :], piece).then_inc(ring_landed[m % RING], 16)

            no_tails = dict.fromkeys(("message", "conv1", "conv1_end", "conv2", "conv2_end", "uv", "uv_end",
                                      "vu", "vu_end", "last"), lambda G, s: {}) | {"start0": {}, "start1": {}}

            def stores_landed():
                for h in range(2):
                    eng.wait_ge(out_stored[h], 16 * SC)

            whole_program(eng, superchunk, no_tails, None, lambda: None, stores_landed)

        @block.scalar
        def _(eng):
            for j in range(HALVES):
                eng.dma_start(xs[:, j * TH:(j + 1) * TH, :],
                              x[j * BANK:(j + 1) * BANK, :].rearrange("(t p) f -> p t f", p=P))\
                   .then_inc(x_landed[j], 16)
            eng.wait_ge(ident_made, 1)
            eng.activation(ident_r[:, :], ident[:, :], ACT.Copy).then_inc(consts_rounded, 1)
            eng.wait_ge(consts_made, 1)
            eng.activation(ones_r[:, :], ones_f[:, :], ACT.Copy).then_inc(consts_rounded, 1)

            eng.wait_ge(w_landed, 16 * WEIGHT_LOADS)

            def split_hi(j, src, func):
                eng.activation(h_hi[:, j * TH:(j + 1) * TH, :], src, func).then_inc(h_hi_ready, 1)

            def normed_hi(j, o):
                eng.wait_ge(normed[j % 2], o + j // 2 + 1)
                split_hi(j, rows[:, j % 2, :, :], ACT.Relu)

            def refilled_hi(kind):
                def steps(base):
                    def step(j):
                        eng.wait_ge(pieces_used, (base + SC - 1) * PER + (j + 1) * TH)
                        G, h = base + j // 2, j % 2
                        if kind == "conv1":
                            eng.wait_ge(scaled[h], G - SC + 1)
                        elif kind == "conv2":
                            eng.wait_ge(normed[h], occurrence(G) + 1)
                        else:
                            eng.wait_ge(act_ready[2][h], mlp_turn(G) + 1)
                        split_hi(j, h_next[:, j * TH:(j + 1) * TH, :], ACT.Relu if kind == "conv2" else ACT.Copy)
                    return {j * TH + 8: [lambda j=j: step(j)] for j in range(HALVES - 2)}
                return steps

            normed_hi(0, 0)

            def superchunk(G, p, s, steps):
                def bulk(k):
                    n = G * PER + k
                    if k in KEPT:
                        if p <= 1:
                            eng.wait_ge(kept_landed[KEPT.index(k)], 16 * (G + 1))
                    else:
                        m = STREAMED.index(k)
                        eng.wait_ge(ring_landed[m % RING],
                                    16 * (G * (len(STREAMED) // RING) + m // RING + 1))
                    if not (isinstance(G, int) and n < HI):
                        eng.wait_ge(pieces_used, n - HI + 1)
                    if p == 0:
                        eng.activation(hi[:, k % HI, :], piece_source(k, s, G), ACT.Copy,
                                       accum_out=row_part[:, k, bass.ds(s, 1)]).then_inc(hi_ready, 1)
                    else:
                        eng.activation(hi[:, k % HI, :], piece_source(k, s, G), ACT.Copy)\
                           .then_inc(hi_ready, 1)
                run(bulk, steps)

            def copy_acc(h, G, s):
                eng.wait_ge(pieces_used, (G + 1) * PER)
                eng.activation(cols[:, h, :, :].rearrange("p q f -> p (q f)"), acc(s % 2, h), ACT.Copy)\
                   .then_inc(acc_copied, 1)

            def copy_norm(h, G, s):
                eng.wait_ge(norm_turned[h], G - SC + 1)
                eng.activation(cols[:, h, :, :].rearrange("p q f -> p (q f)"), tail(h), ACT.Relu)\
                   .then_inc(norm_t_copied[h], 1)

            def scale_hw(end):
                def step(h, G, s):
                    eng.wait_ge(hw_done[h], G - SC + 1)
                    t0 = tile0(G, s, h)
                    for q in range(TH):
                        to = rows[:, h, q, :] if end else \
                            h_next[:, bass.ds(t0 + q, 1), :].rearrange("p a f -> p (a f)")
                        op = eng.activation(to, tail(h, q), ACT.Identity, scale=d_inv2[:, bass.ds(t0 + q, 1)])
                    op.then_inc(scaled[h], 1)
                return step

            def end_hi(ready, count, func):
                def step(h, G, s):
                    eng.wait_ge(ready[h], count(G) + 1)
                    split_hi(HALVES - 2 + h, rows[:, h, :, :], func)
                return step

            def biased(i, kind):
                def step(h, G, s):
                    eng.wait_ge(lin_done[i][h], mlp_turn(G) + 1)
                    to = cols[:, h, :, :].rearrange("p q f -> p (q f)")
                    if i < 2:
                        b = 3 * kind + i
                        eng.activation(to, tail(h), ACT.Identity, bias=mb[:, b:b + 1])\
                           .then_inc(pre_ready[i][h], 1)
                    else:
                        eng.activation(to, tail(h), ACT.Copy).then_inc(pre_ready[i][h], 1)
                return step

            def store_out(h, G, s):
                turn = G - (MLP0 + 2 * ROUNDS) * SC + 1
                eng.wait_ge(out_ready[h], turn)
                eng.dma_start(out[bass.ds(s * WIDE + h * BANK, BANK), :].rearrange("(t p) f -> p t f", p=P),
                              xs[:, bass.ds(tile0(G, s, h), TH), :]).then_inc(out_stored[h], 16)

            def mlp(kind, *more):
                return lambda G, s: slots([(3, 4, copy_acc), (8, 9, biased(0, kind)), (13, 14, biased(1, kind)),
                                           (18, 19, biased(2, kind)), *more], G, s)

            mlp_end = (20, 21, end_hi(act_ready[2], mlp_turn, ACT.Copy))
            tails = {
                "start0": {j * TH - 2: [lambda j=j: normed_hi(j, 0)] for j in range(1, HALVES)},
                "message": lambda G, s: slots([(3, 4, copy_acc)], G, s),
                "start1": {j * TH - 2: [lambda j=j: normed_hi(j, HALVES // 2)] for j in range(1, HALVES)},
                "conv1": lambda G, s: slots([(3, 4, copy_acc), (16, 17, copy_norm), (21, 22, scale_hw(False))], G, s),
                "conv1_end": lambda G, s: slots([(3, 4, copy_acc), (16, 17, copy_norm), (21, 22, scale_hw(True)),
                                                 (21, 22, end_hi(scaled, lambda G: G - SC, ACT.Copy))], G, s),
                "conv2": lambda G, s: slots([(3, 4, copy_acc)], G, s),
                "conv2_end": lambda G, s: slots([(3, 4, copy_acc), (13, 14, end_hi(normed, occurrence, ACT.Relu))],
                                                G, s),
                "uv": mlp(0), "uv_end": mlp(0, mlp_end),
                "vu": mlp(1), "vu_end": mlp(1, mlp_end),
                "last": mlp(0, (21, 22, store_out)),
            }
            refill = {kind: refilled_hi(kind) for kind in ("conv1", "conv2", "uv", "vu")}
            whole_program(eng, superchunk, tails, refill, lambda: normed_hi(0, HALVES // 2), lambda: None)

        @block.vector
        def _(eng):
            eng.memset(ones_f[:, :], 1.0).then_inc(consts_made, 1)
            eng.memset(minus_half[:, :], -0.5).then_inc(consts_made, 1)

            def norm_stats(h, o, src, keep=None):
                for q in range(TH):
                    op = eng.bn_stats(stats[:, h, q, :], src[:, q, :])
                op.then_inc(stats_done[h], 1)
                eng.wait_ge(stats_done[h], o + 1)
                if keep is not None:
                    keep()
                for q in range(TH):
                    op = eng.bn_aggr(mean_var[:, h, q, :], stats[:, h, q, :])
                op.then_inc(aggr_done[h], 1)
                if not (isinstance(o, int) and o == 0):
                    eng.wait_ge(rstd_ready[h], o)
                eng.wait_ge(aggr_done[h], o + 1)
                eng.tensor_scalar(var_eps[:, h, :], mean_var[:, h, :, 1], LN_EPS, None, ALU.add)\
                   .then_inc(var_ready[h], 1)

            def norm_rows(h, src, mean, scale, to=None):
                for q in range(TH):
                    op = eng.tensor_scalar(rows[:, h, q, :] if to is None else to(q), src[:, q, :], mean[:, q:q + 1], scale[:, q:q + 1],
                                           ALU.subtract, ALU.mult)
                op.then_inc(normed[h], 1)

            def split_lo(j, count, src, relu):
                eng.wait_ge(h_hi_ready, count + j + 1)
                part = slice(j * TH, (j + 1) * TH)
                eng.scalar_tensor_tensor(out=h_lo[:, part, :], in0=src, scalar=0.0 if relu else 1.0,
                                         in1=h_hi[:, part, :].bitcast(F32), op0=ALU.max if relu else ALU.mult,
                                         op1=ALU.subtract).then_inc(h_ready, 1)

            def start0_stats(j):
                eng.wait_ge(x_landed[j], 16)
                norm_stats(j % 2, j // 2, xs[:, j * TH:(j + 1) * TH, :])

            def start0_norm(j):
                h = j % 2
                eng.wait_ge(rstd_ready[h], j // 2 + 1)
                if j >= 2:
                    eng.wait_ge(h_ready, j - 1)
                norm_rows(h, xs[:, j * TH:(j + 1) * TH, :], mean_var[:, h, :, 0], rstd[:, h, :])

            def start1_norm(j):
                h, a, b = j % 2, j * TH, (j + 1) * TH
                eng.wait_ge(h_ready, HALVES + j - 1)
                norm_rows(h, xs[:, a:b, :], mean1[:, a:b], scale1[:, a:b])

            def start_lo(j, count):
                split_lo(j, count, rows[:, j % 2, :, :], True)

            def start_steps(stats, norm, count):
                steps = {}
                for j in range(1, HALVES):
                    if stats is not None:
                        steps.setdefault(max(j * TH - 5, 0), []).append(lambda j=j: stats(j))
                    steps.setdefault(j * TH - 3, []).append(lambda j=j: norm(j))
                    steps.setdefault(j * TH - 2, []).append(lambda j=j: start_lo(j, count))
                return steps

            start0_stats(0)
            start0_norm(0)
            start_lo(0, 0)

            def refilled_lo(relu):
                return lambda base: {
                    j * TH + 8: [lambda j=j: split_lo(j, operand_count(base + SC),
                                                      h_next[:, j * TH:(j + 1) * TH, :], relu)]
                    for j in range(HALVES - 2)}

            def end_lo(relu):
                return lambda h, G, s: split_lo(HALVES - 2 + h, operand_count(G + 1), rows[:, h, :, :], relu)

            def superchunk(G, p, s, steps):
                def bulk(k):
                    n = G * PER + k
                    eng.wait_ge(hi_ready, n + 1)
                    if not (isinstance(G, int) and n < LO):
                        eng.wait_ge(pieces_used, n - LO + 1)
                    eng.tensor_tensor(lo[:, k % LO, :], piece_source(k, s, G), hi[:, k % HI, :].bitcast(F32),
                                      ALU.subtract).then_inc(lo_ready, 1)
                run(bulk, steps)

            def take_col_sums(h, G, s):
                eng.wait_ge(pieces_used, (G + 1) * PER)
                if not (isinstance(G, int) and G == 0):
                    eng.wait_ge(x_kept[h], G)
                for q in range(TH):
                    op = eng.scalar_tensor_tensor(out=rows[:, h, q, :], in0=csum(h)[:, q * P:(q + 1) * P],
                                                  scalar=1.0, in1=ident[:, :], op0=ALU.mult, op1=ALU.mult,
                                                  accum_out=col_sum[:, h, q:q + 1])
                op.then_inc(csum_read, 1)

            def invert_col_sums(h, G, s):
                eng.wait_ge(csum_read, 2 * G + h + 1)
                eng.reciprocal(inv_raw[:, h, :], col_sum[:, h, :]).then_inc(inv_step[h], 1)
                eng.wait_ge(inv_step[h], 4 * G + 1)
                eng.tensor_scalar(inv_cap[:, h, :], inv_raw[:, h, :], 3.4028234e38, -3.4028234e38,
                                  ALU.min, ALU.max).then_inc(inv_step[h], 1)
                eng.wait_ge(inv_step[h], 4 * G + 2)
                eng.tensor_tensor(inv_fin[:, h, :], inv_raw[:, h, :], inv_cap[:, h, :], ALU.is_equal)\
                   .then_inc(inv_step[h], 1)
                eng.wait_ge(inv_step[h], 4 * G + 3)
                eng.tensor_tensor(inv_deg[:, h, :], inv_fin[:, h, :], inv_cap[:, h, :], ALU.mult)\
                   .then_inc(inv_step[h], 1)

            def keep_x(h, t0):
                eng.tensor_scalar(xs[:, bass.ds(t0, TH), :], rows[:, h, :, :], 1.0, None, ALU.mult)\
                   .then_inc(x_kept[h], 1)

            def add_message(h, G, s):
                eng.wait_ge(turned[h], G + 1)
                eng.wait_ge(inv_step[h], 4 * G + 4)
                t0 = tile0(G, s, h)
                for q in range(TH):
                    xt = xs[:, bass.ds(t0 + q, 1), :].rearrange("p a f -> p (a f)")
                    op = eng.scalar_tensor_tensor(out=rows[:, h, q, :], in0=tail(h, q),
                                                  scalar=inv_deg[:, h, q:q + 1],
                                                  in1=xt, op0=ALU.mult, op1=ALU.add)
                op.then_inc(x_updated[h], 1)
                eng.wait_ge(x_updated[h], G + 1)
                norm_stats(h, occurrence(G), rows[:, h, :, :], lambda: keep_x(h, t0))
                eng.tensor_copy(mean1[:, bass.ds(t0, TH)], mean_var[:, h, :, 0]).then_inc(mean_kept, 1)

            def boundary():
                eng.tensor_reduce(row_sum[:, :], row_part[:, :, :], AX.X, ALU.add).then_inc(deg_step, 1)
                eng.wait_ge(deg_step, 1)
                eng.tensor_scalar(degree[:, 0, :], row_sum[:, :], 1.0, 1e-8, ALU.add, ALU.add)\
                   .then_inc(deg_ready, 1)
                eng.tensor_scalar(degree[:, 1, :], row_sum[:, :], 1.0, 1.2e-38, ALU.add, ALU.max)\
                   .then_inc(deg_ready, 1)
                eng.tensor_scalar(deg_pos[:, :], row_sum[:, :], 1.0, 0.0, ALU.add, ALU.is_gt)\
                   .then_inc(deg_step, 1)
                eng.wait_ge(deg_step, 2)
                eng.wait_ge(deg_pow_ready, 1)
                eng.tensor_tensor(d_inv2[:, :], deg_pow[:, 1, :], deg_pos[:, :], ALU.mult)\
                   .then_inc(d_inv_ready, 1)
                for h in range(2):
                    eng.wait_ge(rstd_ready[h], HALVES // 2 + SC)
                eng.tensor_tensor(scale1[:, :], rstd1[:, :], d_inv1, ALU.mult).then_inc(d_inv_ready, 1)
                eng.wait_ge(d_inv_ready, 2)
                eng.wait_ge(mean_kept, HALVES)
                start1_norm(0)
                start_lo(0, operand_count(SC))

            def add_conv(scale):
                def step(h, G, s):
                    eng.wait_ge(turned[h], G + 1)
                    t0 = tile0(G, s, h)
                    for q in range(TH):
                        op = eng.tensor_scalar(cols[:, h, q, :], tail(h, q), scale[:, bass.ds(t0 + q, 1)], 0.0,
                                               ALU.mult, ALU.max)
                    op.then_inc(relu_ready[h], 1)
                    eng.wait_ge(relu_ready[h], G - SC + 1)
                    eng.tensor_tensor(rows[:, h, :, :], cols[:, h, :, :], xs[:, bass.ds(t0, TH), :], ALU.add)\
                       .then_inc(x_updated[h], 1)
                return step

            def stats_after(h, G, s):
                eng.wait_ge(x_updated[h], G + 1)
                norm_stats(h, occurrence(G), rows[:, h, :, :], lambda: keep_x(h, tile0(G, s, h)))

            def norm_after(direct):
                def step(h, G, s):
                    eng.wait_ge(rstd_ready[h], occurrence(G) + 1)
                    eng.wait_ge(x_kept[h], G + 1)
                    t0 = tile0(G, s, h)
                    to = None if direct else \
                        (lambda q: h_next[:, bass.ds(t0 + q, 1), :].rearrange("p a f -> p (a f)"))
                    norm_rows(h, rows[:, h, :, :], mean_var[:, h, :, 0], rstd[:, h, :], to)
                return step

            def leaky(i, direct=True):
                def step(h, G, s):
                    eng.wait_ge(pre_ready[i][h], mlp_turn(G) + 1)
                    v = cols[:, h, :, :]
                    to = rows[:, h, :, :] if direct else h_next[:, bass.ds(tile0(G, s, h), TH), :]
                    eng.scalar_tensor_tensor(out=to, in0=v, scalar=SLOPE, in1=v,
                                             op0=ALU.mult, op1=ALU.max).then_inc(act_ready[i][h], 1)
                return step

            def add_out(h, G, s):
                eng.wait_ge(act_ready[2][h], mlp_turn(G) + 1)
                xt = xs[:, bass.ds(tile0(G, s, h), TH), :]
                eng.tensor_tensor(xt, xt, rows[:, h, :, :], ALU.add).then_inc(out_ready[h], 1)

            def mlp(direct, *more):
                return lambda G, s: slots([(8, 9, leaky(0)), (13, 14, leaky(1)), (18, 19, leaky(2, direct)), *more],
                                          G, s)

            def conv(scale, direct, *more):
                return lambda G, s: slots([(8, 9, add_conv(scale)), (9, 10, stats_after),
                                           (11, 12, norm_after(direct)), *more], G, s)

            tails = {
                "start0": start_steps(start0_stats, start0_norm, 0),
                "message": lambda G, s: slots([(1, 1, take_col_sums), (2, 3, invert_col_sums), (8, 10, add_message)],
                                              G, s),
                "start1": start_steps(None, start1_norm, operand_count(SC)),
                "conv1": conv(d_inv1, True),
                "conv1_end": conv(d_inv1, True, (22, 23, end_lo(False))),
                "conv2": conv(d_inv2, False),
                "conv2_end": conv(d_inv2, True, (13, 14, end_lo(True))),
                "uv": mlp(False), "uv_end": mlp(True, (20, 21, end_lo(False))),
                "vu": mlp(False), "vu_end": mlp(True, (20, 21, end_lo(False))),
                "last": mlp(True, (20, 21, add_out)),
            }
            refill = {kind: refilled_lo(kind == "conv2") for kind in ("conv1", "conv2", "uv", "vu")}
            whole_program(eng, superchunk, tails, refill, boundary, lambda: None)

        @block.gpsimd
        def _(eng):
            eng.memset(ident[:, :], 0.0).then_inc(ident_zeroed, 1)
            eng.wait_ge(ident_zeroed, 1)
            eng.affine_select(out=ident[:, :], in_=ident[:, :], compare_op=ALU.not_equal, fill=1.0,
                              base=0, pattern=[[-1, P]], channel_multiplier=1).then_inc(ident_made, 1)
            eng.wait_ge(consts_made, 2)

            def inv_root(h, o, to):
                eng.wait_ge(var_ready[h], o + 1)
                eng.tensor_tensor(to, var_eps[:, h, :], minus_half[:, 0:TH], ALU.pow)\
                   .then_inc(rstd_ready[h], 1)

            for j in range(HALVES):
                if j >= 2:
                    eng.wait_ge(normed[j % 2], j // 2)
                inv_root(j % 2, j // 2, rstd[:, j % 2, :])

            with eng.Fori(0, SC) as s:
                for h in range(2):
                    inv_root(h, occurrence(s), rstd1[:, bass.ds(tile0(s, s, h), TH)])
            eng.wait_ge(deg_ready, 2)
            eng.tensor_tensor(deg_pow[:, :, :].rearrange("p a t -> p (a t)"),
                              degree[:, :, :].rearrange("p a t -> p (a t)"), minus_half[:, :], ALU.pow)\
               .then_inc(deg_pow_ready, 1)
            with eng.Fori(SC, 3 * SC) as G:
                for h in range(2):
                    inv_root(h, occurrence(G), rstd[:, h, :])

        @block.tensor
        def _(eng):
            eng.wait_ge(consts_rounded, 2)
            eng.wait_ge(w_landed, 16 * WEIGHT_LOADS)

            def superchunk(G, p, s, steps):
                a, b = h_hi, h_lo

                def bulk(k):
                    n = G * PER + k
                    first, last = k == 0, k == KT - 1
                    if isinstance(s, int) and s == 0 and k % TH == 0:
                        eng.wait_ge(h_ready, operand_count(G) + (k // TH + 1))
                    if k == 0 and not (isinstance(G, int) and G < 2):
                        eng.wait_ge(acc_copied, 2 * (G - 1))
                    eng.wait_ge(hi_ready, n + 1)
                    for h in range(2):
                        eng.matmul(acc(s % 2, h), b[:, k, :], hi[:, k % HI, h * BANK:(h + 1) * BANK],
                                   start=first, stop=False)
                    for h in range(2):
                        eng.matmul(acc(s % 2, h), a[:, k, :], hi[:, k % HI, h * BANK:(h + 1) * BANK],
                                   start=False, stop=False)
                    if p in (1, 2) and k // (2 * TH) == s:
                        c = (k % TH) * P
                        for w in (b, a):
                            eng.matmul(acc(s % 2, k // TH % 2, c, c + P), w[:, k, :], ident_r[:, :],
                                       start=False, stop=False)
                    eng.wait_ge(lo_ready, n + 1)
                    for h in range(2):
                        op = eng.matmul(acc(s % 2, h), a[:, k, :], lo[:, k % LO, h * BANK:(h + 1) * BANK],
                                        start=False, stop=last)
                    if p == 0:
                        if k == 0 and not (isinstance(G, int) and G == 0):
                            eng.wait_ge(csum_read, 2 * G)
                        for h in range(2):
                            eng.matmul(csum(h), ones_r[:, :], hi[:, k % HI, h * BANK:(h + 1) * BANK],
                                       start=first, stop=False)
                        for h in range(2):
                            op = eng.matmul(csum(h), ones_r[:, :], lo[:, k % LO, h * BANK:(h + 1) * BANK],
                                            start=False, stop=last)
                    op.then_inc(pieces_used, 1)
                run(bulk, steps)

            def turn(h, G, s):
                eng.wait_ge(acc_copied, 2 * G + h + 1)
                for q in range(TH):
                    op = eng.transpose(tail(h, q), cols[:, h, q, :], ident[:, :])
                op.then_inc(turned[h], 1)

            def weigh(h, G, s):
                eng.wait_ge(acc_copied, 2 * G + h + 1)
                for q in range(TH):
                    op = eng.matmul(tail(h, q), cols[:, h, q, :], wl1[:, :], start=True, stop=True)
                op.then_inc(turned[h], 1)

            def turn_norm(h, G, s):
                eng.wait_ge(normed[h], occurrence(G) + 1)
                for q in range(TH):
                    op = eng.transpose(tail(h, q), rows[:, h, q, :], ident[:, :])
                op.then_inc(norm_turned[h], 1)

            def linear_rows(h, w, bias, lhs):
                for q in range(TH):
                    eng.matmul(tail(h, q), lhs[:, h, q, :], w, start=True, stop=False)
                    op = eng.matmul(tail(h, q), ones_f[0:1, :], bias, start=False, stop=True)
                return op

            def second_weight(h, G, s):
                eng.wait_ge(norm_t_copied[h], G - SC + 1)
                linear_rows(h, wl2[:, :], bl2[:, :], cols).then_inc(hw_done[h], 1)

            def layer(i, kind):
                def step(h, G, s):
                    if i == 0:
                        eng.wait_ge(acc_copied, 2 * G + h + 1)
                    else:
                        eng.wait_ge(act_ready[i - 1][h], mlp_turn(G) + 1)
                    w = mw[:, 3 * kind + i, :]
                    if i < 2:
                        src = cols if i == 0 else rows
                        eng.matmul(tail(h), w, src[:, h, :, :].rearrange("p q f -> p (q f)"),
                                   start=True, stop=True).then_inc(lin_done[i][h], 1)
                    else:
                        linear_rows(h, w, mb3[:, kind, :], rows).then_inc(lin_done[i][h], 1)
                return step

            def mlp(kind):
                return lambda G, s: slots([(4, 5, layer(0, kind)), (9, 10, layer(1, kind)),
                                           (14, 15, layer(2, kind))], G, s)

            turning = lambda G, s: slots([(4, 5, turn)], G, s)
            conv1 = lambda G, s: slots([(4, 5, weigh), (12, 13, turn_norm), (17, 18, second_weight)], G, s)
            tails = {
                "start0": {}, "message": turning,
                "start1": {}, "conv1": conv1, "conv1_end": conv1,
                "conv2": turning, "conv2_end": turning,
                "uv": mlp(0), "uv_end": mlp(0), "vu": mlp(1), "vu_end": mlp(1), "last": mlp(0),
            }
            whole_program(eng, superchunk, tails, None, lambda: None, lambda: None, unrolled=True)


_INS = ["x", "adj", "L1_gnn_weight", "L2_gnn_W", "L2_gnn_b"] + [
    f"L3_gnn_{d}_{n}{i}" for d in ("uv", "vu") for n in ("W", "b") for i in (1, 2, 3)]


def kernel(**inputs):
    import numpy as np
    import concourse.bacc as bacc
    from concourse.bass_utils import run_bass_kernel_spmd

    arrays = {name: np.ascontiguousarray(inputs[name]) for name in _INS}
    arrays["adj_t"] = np.ascontiguousarray(np.asarray(inputs["adj"]).T)
    arrays["L2_gnn_W"] = np.ascontiguousarray(np.asarray(inputs["L2_gnn_W"]).T)

    nc = bacc.Bacc("TRN2", target_bir_lowering=False, num_devices=1)
    ap = {name: nc.dram_tensor(f"in_{name}", a.shape, mybir.dt.from_np(a.dtype), kind="ExternalInput").ap()
          for name, a in arrays.items()}
    out = nc.dram_tensor("out_0", (N, P), F32, kind="ExternalOutput").ap()
    build(nc, ap["x"], ap["adj"], ap["adj_t"], ap["L1_gnn_weight"], ap["L2_gnn_W"], ap["L2_gnn_b"],
          [ap[f"L3_gnn_{d}_W{i}"] for d in ("uv", "vu") for i in (1, 2, 3)],
          [ap[f"L3_gnn_{d}_b{i}"] for d in ("uv", "vu") for i in (1, 2, 3)], out)
    result = run_bass_kernel_spmd(nc, [{f"in_{name}": a for name, a in arrays.items()}], core_ids=[0])
    return result.results[0]["out_0"]
```

```python
from contextlib import ExitStack

import concourse.bass as bass
from concourse import mybir

F32 = mybir.dt.float32
F32R = mybir.dt.float32r
ALU = mybir.AluOpType
ACT = mybir.ActivationFunctionType
AX = mybir.AxisListType

P = 128
N = 4096
KT = N // P
BANK = 512
WIDE = 2 * BANK
SC = N // WIDE
TH = BANK // P
HALVES = KT // TH

KEPT = (7, 15, 23, 31)
STREAMED = tuple(k for k in range(KT) if k not in KEPT)
RING = 7
HI = 4
LO = 4
ADDED = ((18,), (0, 2, 4, 6, 8, 10, 13, 18, 21, 23, 25, 27), (0, 2, 4, 6, 8, 14, 19, 23, 25, 27))
SUM_USED = 29
LN_EPS = 1e-5
SLOPE = 0.01
REFILL = (8, 12, 16, 20, 24, 30)
WEIGHT_LOADS = 3 + 2 * 6

MLP0 = 3
ROUNDS = 2


def build(nc, x, adj, adj_t, w_l1, w_l2t, b_l2, mlp_w, mlp_b, out):
    with ExitStack() as ctx:
        def sb(name, shape, dt=F32):
            return ctx.enter_context(nc.sbuf_tensor(name, shape, dt))

        def sem(name):
            return ctx.enter_context(nc.semaphore(name))

        def sems(name, n):
            return [sem(f"{name}{i}") for i in range(n)]

        kept = sb("kept", [P, SC * len(KEPT), WIDE])
        ring = sb("ring", [P, RING, WIDE])
        hi = sb("hi", [P, HI, WIDE], F32R)
        lo = sb("lo", [P, LO, WIDE], F32R)
        piece_sum = sb("piece_sum", [P, WIDE])
        h_hi = sb("h_hi", [P, KT, P], F32R)
        h_lo = sb("h_lo", [P, KT, P], F32R)
        h_next = sb("h_next", [P, KT - 2 * TH, P])
        xs = sb("xs", [P, KT, P])
        cols = sb("cols", [P, 2, TH, P])
        rows = sb("rows", [P, 2, TH, P])
        wl1 = sb("wl1", [P, P])
        wl2 = sb("wl2", [P, P])
        bl2 = sb("bl2", [1, P])
        bl2_hi = sb("bl2_hi", [1, P], F32R)
        bl2_lo = sb("bl2_lo", [1, P], F32R)
        mw = sb("mw", [P, 6, P])
        mb = sb("mb", [P, 6])
        ident = sb("ident", [P, P])
        ident_r = sb("ident_r", [P, P], F32R)
        ones_r = sb("ones_r", [P, P], F32R)
        ones_f = sb("ones_f", [P, P])
        stats = sb("stats", [P, 2, TH, 6])
        mean_var = sb("mean_var", [P, 2, TH, 2])
        var_eps = sb("var_eps", [P, 2, TH])
        rstd = sb("rstd", [P, 2, TH])
        minus_half = sb("minus_half", [P, 2 * TH])
        csum_rows = sb("csum_rows", [P, 2, P])
        inv_raw = sb("inv_raw", [P, 2, TH])
        inv_cap = sb("inv_cap", [P, 2, TH])
        inv_fin = sb("inv_fin", [P, 2, TH])
        inv_deg = sb("inv_deg", [P, 2, TH])
        row_part = sb("row_part", [P, KT, SC])
        row_sum = sb("row_sum", [P, KT])
        degree = sb("degree", [P, KT, 2])
        deg_pow = sb("deg_pow", [P, KT, 2])
        deg_pos = sb("deg_pos", [P, KT])
        d_inv1 = deg_pow[:, :, 0]
        d_inv2 = sb("d_inv2", [P, KT])

        ps = ctx.enter_context(nc.psum_tensor("ps", [P, 8 * BANK], F32))

        def acc(parity, h, a=0, b=BANK):
            return ps[:, bass.ds((parity * 2 + h) * BANK + a, b - a)]

        def csum(h):
            return ps[:, (4 + h) * BANK:(5 + h) * BANK]

        def tail(h, q=None):
            base = (6 + h) * BANK
            return ps[:, base:base + BANK] if q is None else ps[:, base + q * P:base + (q + 1) * P]

        x_landed = sems("x_landed", HALVES)
        w_landed = sem("w_landed")
        bias_split = sem("bias_split")
        ident_zeroed = sem("ident_zeroed")
        ident_made = sem("ident_made")
        consts_made = sem("consts_made")
        consts_rounded = sem("consts_rounded")
        ring_landed = sems("ring_landed", RING)
        kept_landed = sems("kept_landed", len(KEPT))
        kept_t_landed = sems("kept_t_landed", len(KEPT))
        hi_ready = sem("hi_ready")
        lo_ready = sem("lo_ready")
        piece_added = sem("piece_added")
        pieces_used = sem("pieces_used")
        h_hi_ready = sem("h_hi_ready")
        h_ready = sem("h_ready")
        acc_copied = sem("acc_copied")
        csum_copied = sem("csum_copied")
        csum_turned = sems("csum_turned", 2)
        stats_done = sems("stats_done", 2)
        aggr_done = sems("aggr_done", 2)
        var_ready = sems("var_ready", 2)
        rstd_ready = sems("rstd_ready", 2)
        normed = sems("normed", 2)
        x_updated = sems("x_updated", 2)
        x_kept = sems("x_kept", 2)
        inv_step = sems("inv_step", 2)
        turned = sems("turned", 2)
        relu_ready = sems("relu_ready", 2)
        norm_turned = sems("norm_turned", 2)
        norm_t_copied = sems("norm_t_copied", 2)
        hw_done = sems("hw_done", 2)
        conv_next_ready = sems("conv_next_ready", 2)
        lin_done = [sems(f"lin{i}_done", 2) for i in (1, 2)]
        pre_ready = [sems(f"pre{i}_ready", 2) for i in (1, 2)]
        act_ready = [sems(f"act{i}_ready", 2) for i in range(3)]
        v_turned = sems("v_turned", 2)
        next_ready = sems("next_ready", 2)
        deg_summed = sem("deg_summed")
        deg_ready = sem("deg_ready")
        deg_pow_ready = sem("deg_pow_ready")
        weighted = sem("weighted")
        out_ready = sems("out_ready", 2)
        out_stored = sems("out_stored", 2)

        PER = KT

        def norm_turn(G):
            return HALVES // 2 + G

        def tile0(G, s, h):
            return s * (2 * TH) + h * TH

        def run(bulk, steps):
            for k in range(KT):
                if bulk is not None:
                    bulk(k)
                for step in steps.get(k, ()):
                    step()

        def slots(table, *args):
            steps = {}
            for a, b, f in table:
                for h, k in ((0, a), (1, b)):
                    steps.setdefault(k, []).append(lambda f=f, h=h: f(h, *args))
            return steps

        def joined(first, second):
            return {k: first.get(k, []) + second.get(k, []) for k in first.keys() | second.keys()}

        def whole_program(eng, superchunk, tails, refill, between, last_tail, unrolled=False):
            def rest(base, p, kind):
                if unrolled and p in (1, 2):
                    for s in range(1, SC):
                        superchunk(base + s, p, s, tails[kind](base + s - 1, s - 1))
                    return
                if refill is None:
                    with eng.Fori(1, SC) as s:
                        superchunk(base + s, p, s, tails[kind](base + s - 1, s - 1))
                    return
                with eng.Fori(1, SC - 1) as s:
                    superchunk(base + s, p, s, tails[kind](base + s - 1, s - 1))
                superchunk(base + SC - 1, p, SC - 1,
                           joined(tails[kind](base + SC - 2, SC - 2), refill[kind](base)))

            superchunk(0, 0, 0, tails["start0"])
            rest(0, 0, "message")
            between()
            superchunk(SC, 1, 0, tails["message_end"](SC - 1, SC - 1))
            rest(SC, 1, "conv1")
            superchunk(2 * SC, 2, 0, tails["conv1_end"](2 * SC - 1, SC - 1))
            rest(2 * SC, 2, "conv2")
            superchunk(3 * SC, 3, 0, tails["conv2_end"](3 * SC - 1, SC - 1))
            with eng.Fori(0, ROUNDS) as r:
                base = MLP0 * SC + r * (2 * SC)
                rest(base, 3, "uv")
                superchunk(base + SC, 4, 0, tails["uv_end"](base + SC - 1, SC - 1))
                rest(base + SC, 4, "vu")
                superchunk(base + 2 * SC, 5, 0, tails["vu_end"](base + 2 * SC - 1, SC - 1))
            base = (MLP0 + 2 * ROUNDS) * SC
            with eng.Fori(1, SC) as s:
                superchunk(base + s, 7, s, tails["last"](base + s - 1, s - 1))
            run(None, tails["last"](base + SC - 1, SC - 1))
            last_tail()

        def next_count(base, s):
            return mlp_turn(base) * (SC - 1) + SC * (s + 1)

        def added_pieces(G):
            if isinstance(G, int) and G == 0:
                return ADDED[0], 0
            if isinstance(G, int) and G == SC - 1:
                return ADDED[2], len(ADDED[0]) + (SC - 2) * len(ADDED[1])
            return ADDED[1], len(ADDED[0]) + (G - 1) * len(ADDED[1])

        def operand_count(G):
            return 2 * G

        def mlp_turn(G):
            return G - MLP0 * SC

        def piece_source(k, s, G):
            if k in KEPT:
                return kept[:, bass.ds(s * len(KEPT) + KEPT.index(k), 1), :].rearrange("p a n -> p (a n)")
            return ring[:, STREAMED.index(k) % RING, :]

        def load_x(eng, j):
            eng.dma_start(xs[:, j * TH:(j + 1) * TH, :],
                          x[j * BANK:(j + 1) * BANK, :].rearrange("(t p) f -> p t f", p=P))\
               .then_inc(x_landed[j], 16)

        block = ctx.enter_context(nc.Block())

        @block.sync
        def _(eng):
            load_x(eng, 0)

            def kept_place(s, k):
                return kept[:, bass.ds(s * len(KEPT) + KEPT.index(k), 1), :].rearrange("p a n -> p (a n)")

            def superchunk(G, p, s, steps):
                src = adj if p == 0 else adj_t
                for k in range(KT):
                    piece = src[k * P:(k + 1) * P, bass.ds(s * WIDE, WIDE)]
                    if k in KEPT:
                        i = KEPT.index(k)
                        if p == 0:
                            eng.dma_start(kept_place(s, k), piece).then_inc(kept_landed[i], 16)
                        if p == 0 and not isinstance(s, int) or p == 1 and isinstance(s, int):
                            eng.wait_ge(lo_ready, (G - 1) * PER + k + 1)
                            b = (G - 1) if p == 1 else (s - 1)
                            eng.dma_start(kept_place(b, k), adj_t[k * P:(k + 1) * P, bass.ds(b * WIDE, WIDE)])\
                               .then_inc(kept_t_landed[i], 16)
                        continue
                    m = STREAMED.index(k)
                    if m >= RING:
                        eng.wait_ge(lo_ready, G * PER + STREAMED[m - RING] + 1)
                    elif not (isinstance(G, int) and G == 0):
                        eng.wait_ge(lo_ready, (G - 1) * PER + STREAMED[len(STREAMED) + m - RING] + 1)
                    eng.dma_start(ring[:, m % RING, :], piece).then_inc(ring_landed[m % RING], 16)

            no_tails = dict.fromkeys(("message", "message_end", "conv1", "conv1_end", "conv2", "conv2_end",
                                      "uv", "uv_end", "vu", "vu_end", "last"), lambda G, s: {}) | {"start0": {}}

            def stores_landed():
                for h in range(2):
                    eng.wait_ge(out_stored[h], 16 * SC)

            whole_program(eng, superchunk, no_tails, None, lambda: None, stores_landed)

        @block.scalar
        def _(eng):
            eng.wait_ge(ident_made, 1)
            eng.activation(ident_r[:, :], ident[:, :], ACT.Copy).then_inc(consts_rounded, 1)
            eng.wait_ge(consts_made, 2)
            eng.activation(ones_r[:, :], ones_f[:, :], ACT.Copy).then_inc(consts_rounded, 1)
            load_x(eng, 1)
            load_x(eng, 2)

            def split_hi(j, src, func):
                eng.activation(h_hi[:, j * TH:(j + 1) * TH, :], src, func).then_inc(h_hi_ready, 1)

            def normed_hi(j, o):
                if j + 3 < HALVES:
                    load_x(eng, j + 3)
                eng.wait_ge(normed[j % 2], o + j // 2 + 1)
                split_hi(j, rows[:, j % 2, :, :], ACT.Relu)

            def weigh_rows(j, y):
                eng.wait_ge(deg_pow_ready, j + 1)
                eng.wait_ge(normed[j % 2], norm_turn(j // 2) + 1)
                for q in range(TH):
                    t = j * TH + q
                    op = eng.activation(y[:, q, :], y[:, q, :], ACT.Relu, scale=d_inv1[:, t:t + 1])
                op.then_inc(weighted, 1)
                eng.wait_ge(weighted, j + 1)

            def refilled_hi(kind):
                def steps(base):
                    def step(j):
                        eng.wait_ge(pieces_used, (base + SC - 1) * PER + (j + 1) * TH)
                        G, h = base + j // 2, j % 2
                        if kind == "message":
                            weigh_rows(j, h_next[:, j * TH:(j + 1) * TH, :])
                        elif kind == "conv":
                            eng.wait_ge(conv_next_ready[h], G - SC + 1)
                        else:
                            eng.wait_ge(next_ready[h], next_count(base, j // 2))
                        split_hi(j, h_next[:, j * TH:(j + 1) * TH, :], ACT.Copy)
                    return {REFILL[j]: [lambda j=j: step(j)] for j in range(HALVES - 2)}
                return steps

            def superchunk(G, p, s, steps):
                def bulk(k):
                    n = G * PER + k
                    if k in KEPT:
                        if p == 0:
                            eng.wait_ge(kept_landed[KEPT.index(k)], 16 * (G + 1))
                        elif p == 1:
                            eng.wait_ge(kept_t_landed[KEPT.index(k)], 16 * (s + 1))
                    else:
                        m = STREAMED.index(k)
                        eng.wait_ge(ring_landed[m % RING],
                                    16 * (G * (len(STREAMED) // RING) + m // RING + 1))
                    if not (isinstance(G, int) and n < HI):
                        eng.wait_ge(pieces_used, n - HI + 1)
                    if p == 0:
                        eng.activation(hi[:, k % HI, :], piece_source(k, s, G), ACT.Copy,
                                       accum_out=row_part[:, k, bass.ds(s, 1)]).then_inc(hi_ready, 1)
                    else:
                        eng.activation(hi[:, k % HI, :], piece_source(k, s, G), ACT.Copy)\
                           .then_inc(hi_ready, 1)
                run(bulk, steps)

            def copy_acc(h, G, s):
                eng.wait_ge(pieces_used, (G + 1) * PER)
                eng.activation(cols[:, h, :, :].rearrange("p q f -> p (q f)"), acc(s % 2, h), ACT.Copy)\
                   .then_inc(acc_copied, 1)

            def copy_csum(h, G, s):
                eng.wait_ge(pieces_used, (G + 1) * PER)
                for q in range(TH):
                    row = q * (P // TH)
                    op = eng.activation(csum_rows[row:row + 1, h, :],
                                        csum(h)[row:row + 1, q * P:(q + 1) * P], ACT.Copy)
                op.then_inc(csum_copied, 1)

            def copy_norm(h, G, s):
                eng.wait_ge(norm_turned[h], G - SC + 1)
                eng.activation(cols[:, h, :, :].rearrange("p q f -> p (q f)"), tail(h), ACT.Relu)\
                   .then_inc(norm_t_copied[h], 1)

            def scale_hw(end):
                def step(h, G, s):
                    eng.wait_ge(hw_done[h], G - SC + 1)
                    t0 = tile0(G, s, h)
                    for q in range(TH):
                        to = rows[:, h, q, :] if end else \
                            h_next[:, bass.ds(t0 + q, 1), :].rearrange("p a f -> p (a f)")
                        op = eng.activation(to, tail(h, q), ACT.Identity, scale=d_inv2[:, bass.ds(t0 + q, 1)])
                    op.then_inc(conv_next_ready[h], 1)
                return step

            def scaled_hi(h, G, s):
                eng.wait_ge(conv_next_ready[h], G - SC + 1)
                split_hi(HALVES - 2 + h, rows[:, h, :, :], ACT.Copy)

            def weighted_hi(h, G, s):
                weigh_rows(HALVES - 2 + h, rows[:, h, :, :])
                split_hi(HALVES - 2 + h, rows[:, h, :, :], ACT.Copy)

            def tail_hi(ready, count):
                def step(h, G, s):
                    eng.wait_ge(ready[h], count(G) + 1)
                    split_hi(HALVES - 2 + h, tail(h).rearrange("p (q f) -> p q f", q=TH), ACT.Copy)
                return step

            def store_next(ready, count, stored, by):
                def step(h, G, s):
                    eng.wait_ge(ready[h], count(G) + 1)
                    eng.activation(h_next[:, bass.ds(tile0(G, s, h), TH), :],
                                   tail(h).rearrange("p (q f) -> p q f", q=TH), ACT.Copy).then_inc(stored[h], by)
                return step

            def relu_scaled(d_inv):
                def step(h, G, s):
                    eng.wait_ge(turned[h], G + 1)
                    t0 = tile0(G, s, h)
                    for q in range(TH):
                        op = eng.activation(cols[:, h, q, :], tail(h, q), ACT.Relu,
                                            scale=d_inv[:, bass.ds(t0 + q, 1)])
                    op.then_inc(relu_ready[h], 1)
                return step

            def biased(i, kind):
                def step(h, G, s):
                    if i == 0:
                        eng.wait_ge(pieces_used, (G + 1) * PER)
                    else:
                        eng.wait_ge(lin_done[i - 1][h], mlp_turn(G) + 1)
                    b = 3 * kind + i
                    op = eng.activation(cols[:, h, :, :].rearrange("p q f -> p (q f)"),
                                        acc(s % 2, h) if i == 0 else tail(h), ACT.Identity, bias=mb[:, b:b + 1])
                    op.then_inc(acc_copied if i == 0 else pre_ready[i - 1][h], 1)
                return step

            def store_out(h, G, s):
                turn = G - (MLP0 + 2 * ROUNDS) * SC + 1
                eng.wait_ge(out_ready[h], turn)
                eng.dma_start(out[bass.ds(s * WIDE + h * BANK, BANK), :].rearrange("(t p) f -> p t f", p=P),
                              xs[:, bass.ds(tile0(G, s, h), TH), :]).then_inc(out_stored[h], 16)

            def mlp(kind, *more):
                return lambda G, s: slots([(3, 5, biased(0, kind)), (9, 11, biased(1, kind)),
                                           (15, 17, biased(2, kind)), *more], G, s)

            def conv(d_inv, *more):
                return lambda G, s: slots([(3, 4, copy_acc), (6, 14, relu_scaled(d_inv)), (15, 24, copy_norm), *more],
                                          G, s)

            def conv_end(d_inv, *more):
                return lambda G, s: slots([(3, 4, copy_acc), (6, 12, relu_scaled(d_inv)), (15, 21, copy_norm), *more],
                                          G, s)

            conv_turn = lambda G: G - SC
            message = [(3, 3, copy_csum), (3, 4, copy_acc)]
            mlp_store = store_next(v_turned, mlp_turn, next_ready, SC)
            mlp_hi = tail_hi(v_turned, mlp_turn)
            tails = {
                "start0": {max(j * TH - 2, 0): [lambda j=j: normed_hi(j, 0)] for j in range(HALVES)},
                "message": lambda G, s: slots(message, G, s),
                "message_end": lambda G, s: slots([*message, (16, 23, weighted_hi)], G, s),
                "conv1": conv(d_inv1, (19, 28, scale_hw(False))),
                "conv1_end": conv_end(d_inv1, (19, 25, scale_hw(True)), (20, 26, scaled_hi)),
                "conv2": conv(d_inv2, (19, 28, store_next(hw_done, conv_turn, conv_next_ready, 1))),
                "conv2_end": conv_end(d_inv2, (19, 25, tail_hi(hw_done, conv_turn))),
                "uv": mlp(0, (21, 23, mlp_store)), "uv_end": mlp(0, (21, 23, mlp_hi)),
                "vu": mlp(1, (21, 23, mlp_store)), "vu_end": mlp(1, (21, 23, mlp_hi)),
                "last": mlp(0, (22, 24, store_out)),
            }
            refill = {kind: refilled_hi(of) for kind, of in (("message", "message"), ("conv1", "conv"),
                                                             ("conv2", "conv"), ("uv", "mlp"), ("vu", "mlp"))}
            def weights_here():
                eng.wait_ge(w_landed, 16 * WEIGHT_LOADS)
                eng.activation(bl2_hi[:, :], bl2[:, :], ACT.Copy).then_inc(bias_split, 1)

            whole_program(eng, superchunk, tails, refill, weights_here, lambda: None)

        @block.vector
        def _(eng):
            eng.memset(csum_rows[:, :, :], 0.0).then_inc(consts_made, 1)
            eng.memset(ones_f[:, :], 1.0).then_inc(consts_made, 1)
            eng.memset(minus_half[:, :], -0.5).then_inc(consts_made, 1)

            def norm_stats(h, o, src):
                for q in range(TH):
                    op = eng.bn_stats(stats[:, h, q, :], src[:, q, :])
                op.then_inc(stats_done[h], 1)

            def norm_aggr(h, o, t0=None):
                eng.wait_ge(stats_done[h], o + 1)
                if t0 is not None:
                    eng.tensor_scalar(xs[:, bass.ds(t0, TH), :], rows[:, h, :, :], 1.0, None, ALU.mult)\
                       .then_inc(x_kept[h], 1)
                for q in range(TH):
                    op = eng.bn_aggr(mean_var[:, h, q, :], stats[:, h, q, :])
                op.then_inc(aggr_done[h], 1)
                if not (isinstance(o, int) and o == 0):
                    eng.wait_ge(rstd_ready[h], o)
                eng.wait_ge(aggr_done[h], o + 1)
                eng.tensor_scalar(var_eps[:, h, :], mean_var[:, h, :, 1], LN_EPS, None, ALU.add)\
                   .then_inc(var_ready[h], 1)

            def norm_rows(h, src, mean, scale, to=None):
                for q in range(TH):
                    op = eng.tensor_scalar(rows[:, h, q, :] if to is None else to(q), src[:, q, :],
                                           mean[:, q:q + 1], scale[:, q:q + 1],
                                           ALU.subtract, ALU.mult)
                op.then_inc(normed[h], 1)

            def split_lo(j, count, src, relu=False):
                eng.wait_ge(h_hi_ready, count + j + 1)
                part = slice(j * TH, (j + 1) * TH)
                eng.scalar_tensor_tensor(out=h_lo[:, part, :], in0=src, scalar=0.0 if relu else 1.0,
                                         in1=h_hi[:, part, :].bitcast(F32), op0=ALU.max if relu else ALU.mult,
                                         op1=ALU.subtract).then_inc(h_ready, 1)

            def start0_stats(j):
                eng.wait_ge(x_landed[j], 16)
                norm_stats(j % 2, j // 2, xs[:, j * TH:(j + 1) * TH, :])
                norm_aggr(j % 2, j // 2)

            def start0_norm(j):
                h = j % 2
                eng.wait_ge(rstd_ready[h], j // 2 + 1)
                if j >= 2:
                    eng.wait_ge(h_ready, j - 1)
                norm_rows(h, xs[:, j * TH:(j + 1) * TH, :], mean_var[:, h, :, 0], rstd[:, h, :])

            def start_lo(j):
                split_lo(j, 0, rows[:, j % 2, :, :], True)

            def start_steps():
                steps = {}
                for j in range(1, HALVES):
                    for slot, step in ((max(j * TH - 6, 0), start0_stats), (max(j * TH - 4, 1), start0_norm),
                                       (j * TH - 1, start_lo)):
                        steps.setdefault(slot, []).append(lambda j=j, step=step: step(j))
                return steps

            start0_stats(0)
            start0_norm(0)
            start_lo(0)

            def refilled_lo(base):
                return {REFILL[j]: [lambda j=j: split_lo(j, operand_count(base + SC),
                                                          h_next[:, j * TH:(j + 1) * TH, :])]
                        for j in range(HALVES - 2)}

            def end_lo(h, G, s):
                split_lo(HALVES - 2 + h, operand_count(G + 1), rows[:, h, :, :])

            def tail_lo(h, G, s):
                split_lo(HALVES - 2 + h, operand_count(G + 1), tail(h).rearrange("p (q f) -> p q f", q=TH))

            def superchunk(G, p, s, steps):
                def bulk(k):
                    n = G * PER + k
                    eng.wait_ge(hi_ready, n + 1)
                    if not (isinstance(G, int) and n < LO):
                        eng.wait_ge(pieces_used, n - LO + 1)
                    added, before = added_pieces(G) if p == 0 else ((), 0)
                    if k in added:
                        i = added.index(k)
                        piece = piece_source(k, s, G)
                        if i == 0:
                            if not (isinstance(G, int) and G == 0):
                                eng.wait_ge(pieces_used, (G - 1) * PER + SUM_USED + 1)
                            eng.tensor_scalar(piece_sum[:, :], piece, 1.0, None, ALU.mult).then_inc(piece_added, 1)
                        else:
                            eng.wait_ge(piece_added, before + i)
                            eng.tensor_tensor(piece_sum[:, :], piece_sum[:, :], piece, ALU.add)\
                               .then_inc(piece_added, 1)
                    eng.tensor_tensor(lo[:, k % LO, :], piece_source(k, s, G), hi[:, k % HI, :].bitcast(F32),
                                      ALU.subtract).then_inc(lo_ready, 1)
                run(bulk, steps)

            def invert_col_sums(h, G, s):
                eng.wait_ge(csum_turned[h], G + 1)
                eng.reciprocal(inv_raw[:, h, :], tail(h)[:, 0:TH]).then_inc(inv_step[h], 1)
                eng.wait_ge(inv_step[h], 4 * G + 1)
                eng.tensor_scalar(inv_cap[:, h, :], inv_raw[:, h, :], 3.4028234e38, -3.4028234e38,
                                  ALU.min, ALU.max).then_inc(inv_step[h], 1)
                eng.wait_ge(inv_step[h], 4 * G + 2)
                eng.tensor_tensor(inv_fin[:, h, :], inv_raw[:, h, :], inv_cap[:, h, :], ALU.is_equal)\
                   .then_inc(inv_step[h], 1)
                eng.wait_ge(inv_step[h], 4 * G + 3)
                eng.tensor_tensor(inv_deg[:, h, :], inv_fin[:, h, :], inv_cap[:, h, :], ALU.mult)\
                   .then_inc(inv_step[h], 1)

            def add_message(h, G, s):
                eng.wait_ge(turned[h], G + 1)
                eng.wait_ge(inv_step[h], 4 * G + 4)
                t0 = tile0(G, s, h)
                for q in range(TH):
                    xt = xs[:, bass.ds(t0 + q, 1), :].rearrange("p a f -> p (a f)")
                    op = eng.scalar_tensor_tensor(out=rows[:, h, q, :], in0=tail(h, q),
                                                  scalar=inv_deg[:, h, q:q + 1],
                                                  in1=xt, op0=ALU.mult, op1=ALU.add)
                op.then_inc(x_updated[h], 1)

            def sum_degrees(j):
                part = slice(j * TH, (j + 1) * TH)
                eng.tensor_reduce(row_sum[:, part], row_part[:, part, :], AX.X, ALU.add).then_inc(deg_summed, 1)
                eng.wait_ge(deg_summed, j + 1)
                eng.tensor_scalar(degree[:, part, 0], row_sum[:, part], 1.0, 1e-8, ALU.add, ALU.add)
                eng.tensor_scalar(degree[:, part, 1], row_sum[:, part], 1.0, 1.2e-38, ALU.add, ALU.max)
                eng.tensor_scalar(deg_pos[:, part], row_sum[:, part], 1.0, 0.0, ALU.add, ALU.is_gt)\
                   .then_inc(deg_ready, 1)

            def weigh_degrees(j):
                part = slice(j * TH, (j + 1) * TH)
                eng.wait_ge(deg_pow_ready, j + 1)
                eng.wait_ge(deg_ready, j + 1)
                eng.tensor_tensor(d_inv2[:, part], deg_pow[:, part, 1], deg_pos[:, part], ALU.mult)

            def refilled_message(base):
                steps = {}
                for j in range(HALVES):
                    steps[j * TH + 3] = [lambda j=j: sum_degrees(j)]
                for j in range(HALVES - 1):
                    steps[j * TH + 6] = [lambda j=j: weigh_degrees(j)]
                return joined(steps, refilled_lo(base))

            def add_conv(h, G, s):
                eng.wait_ge(relu_ready[h], G - SC + 1)
                eng.tensor_tensor(rows[:, h, :, :], cols[:, h, :, :], xs[:, bass.ds(tile0(G, s, h), TH), :], ALU.add)\
                   .then_inc(x_updated[h], 1)

            def stats_after(h, G, s):
                eng.wait_ge(x_updated[h], G + 1)
                norm_stats(h, norm_turn(G), rows[:, h, :, :])

            def aggr_after(h, G, s):
                norm_aggr(h, norm_turn(G), tile0(G, s, h))

            def norm_after(direct):
                def step(h, G, s):
                    eng.wait_ge(rstd_ready[h], norm_turn(G) + 1)
                    eng.wait_ge(x_kept[h], G + 1)
                    t0 = tile0(G, s, h)
                    to = None if direct else \
                        (lambda q: h_next[:, bass.ds(t0 + q, 1), :].rearrange("p a f -> p (a f)"))
                    norm_rows(h, rows[:, h, :, :], mean_var[:, h, :, 0], rstd[:, h, :], to)
                return step

            def leaky(i):
                def step(h, G, s):
                    if i == 0:
                        eng.wait_ge(acc_copied, 2 * G + h + 1)
                    else:
                        eng.wait_ge(pre_ready[i - 1][h], mlp_turn(G) + 1)
                    v = cols[:, h, :, :]
                    eng.scalar_tensor_tensor(out=rows[:, h, :, :], in0=v, scalar=SLOPE, in1=v,
                                             op0=ALU.mult, op1=ALU.max).then_inc(act_ready[i][h], 1)
                return step

            def add_out(h, G, s):
                eng.wait_ge(v_turned[h], mlp_turn(G) + 1)
                xt = xs[:, bass.ds(tile0(G, s, h), TH), :]
                eng.tensor_tensor(xt, tail(h).rearrange("p (q f) -> p q f", q=TH), xt, ALU.add)\
                   .then_inc(out_ready[h], 1)

            def mlp(*more):
                return lambda G, s: slots([(4, 6, leaky(0)), (10, 12, leaky(1)), (16, 18, leaky(2)), *more], G, s)

            def message(direct, *more):
                return lambda G, s: slots([(5, 6, invert_col_sums), (9, 15, add_message), (10, 16, stats_after),
                                           (11, 17, aggr_after), (13, 20, norm_after(direct)), *more], G, s)

            def conv(G, s):
                return slots([(7, 15, add_conv), (8, 16, stats_after), (9, 17, aggr_after),
                              (11, 20, norm_after(True))], G, s)

            def conv_end(lo):
                return lambda G, s: slots([(7, 13, add_conv), (8, 14, stats_after), (9, 15, aggr_after),
                                           (11, 17, norm_after(True)), (20, 26, lo)], G, s)

            tails = {
                "start0": start_steps(),
                "message": message(False), "message_end": lambda G, s: joined(
                    message(True, (18, 25, end_lo))(G, s), {1: [lambda: weigh_degrees(HALVES - 1)]}),
                "conv1": conv, "conv1_end": conv_end(end_lo),
                "conv2": conv, "conv2_end": conv_end(tail_lo),
                "uv": mlp(), "uv_end": mlp((21, 23, tail_lo)),
                "vu": mlp(), "vu_end": mlp((21, 23, tail_lo)),
                "last": mlp((21, 23, add_out)),
            }
            refill = {kind: refilled_lo for kind in ("conv1", "conv2", "uv", "vu")}
            refill["message"] = refilled_message
            def split_bias():
                eng.wait_ge(bias_split, 1)
                eng.tensor_tensor(bl2_lo[:, :], bl2[:, :], bl2_hi[:, :].bitcast(F32), ALU.subtract)\
                   .then_inc(bias_split, 1)

            whole_program(eng, superchunk, tails, refill, split_bias, lambda: None)

        @block.gpsimd
        def _(eng):
            eng.memset(ident[:, :], 0.0).then_inc(ident_zeroed, 1)
            eng.wait_ge(ident_zeroed, 1)
            eng.affine_select(out=ident[:, :], in_=ident[:, :], compare_op=ALU.not_equal, fill=1.0,
                              base=0, pattern=[[-1, P]], channel_multiplier=1).then_inc(ident_made, 1)
            eng.wait_ge(consts_made, 3)

            def inv_root(h, o, to):
                eng.wait_ge(var_ready[h], o + 1)
                eng.tensor_tensor(to, var_eps[:, h, :], minus_half[:, 0:TH], ALU.pow)\
                   .then_inc(rstd_ready[h], 1)

            for j in range(HALVES):
                if j >= 2:
                    eng.wait_ge(normed[j % 2], j // 2)
                inv_root(j % 2, j // 2, rstd[:, j % 2, :])

            eng.dma_start(wl1[:, :], w_l1).then_inc(w_landed, 16)
            eng.dma_start(wl2[:, :], w_l2t).then_inc(w_landed, 16)
            eng.dma_start(bl2[:, :], b_l2.rearrange("(a f) -> a f", a=1)).then_inc(w_landed, 16)
            for i in range(6):
                eng.dma_start(mw[:, i, :], mlp_w[i]).then_inc(w_landed, 16)
                eng.dma_start(mb[:, i:i + 1], mlp_b[i].rearrange("(f a) -> f a", a=1)).then_inc(w_landed, 16)

            def inv_root_degrees(j):
                part = slice(j * TH, (j + 1) * TH)
                eng.wait_ge(deg_ready, j + 1)
                eng.tensor_tensor(deg_pow[:, part, :].rearrange("p t a -> p (t a)"),
                                  degree[:, part, :].rearrange("p t a -> p (t a)"), minus_half[:, :], ALU.pow)\
                   .then_inc(deg_pow_ready, 1)

            with eng.Fori(0, SC - 2) as G:
                for h in range(2):
                    inv_root(h, norm_turn(G), rstd[:, h, :])
            for j in range(2):
                inv_root_degrees(j)
            inv_root(0, norm_turn(SC - 2), rstd[:, 0, :])
            for j in range(2, 4):
                inv_root_degrees(j)
            inv_root(1, norm_turn(SC - 2), rstd[:, 1, :])
            for j in range(4, HALVES):
                inv_root_degrees(j)
            with eng.Fori(SC - 1, 3 * SC) as G:
                for h in range(2):
                    inv_root(h, norm_turn(G), rstd[:, h, :])

        @block.tensor
        def _(eng):
            eng.wait_ge(consts_rounded, 2)

            def superchunk(G, p, s, steps):
                a, b = h_hi, h_lo
                added, before = added_pieces(G) if p == 0 else ((), 0)
                first_summed = min(set(range(KT)) - set(added))

                def bulk(k):
                    n = G * PER + k
                    first, last = k == 0, k == KT - 1
                    if isinstance(s, int) and s == 0 and k % TH == 0:
                        eng.wait_ge(h_ready, operand_count(G) + (k // TH + 1))
                    if k == 0 and not (isinstance(G, int) and G < 2):
                        eng.wait_ge(acc_copied, 2 * (G - 1))
                    eng.wait_ge(hi_ready, n + 1)
                    for h in range(2):
                        eng.matmul(acc(s % 2, h), b[:, k, :], hi[:, k % HI, h * BANK:(h + 1) * BANK],
                                   start=first, stop=False)
                    for h in range(2):
                        eng.matmul(acc(s % 2, h), a[:, k, :], hi[:, k % HI, h * BANK:(h + 1) * BANK],
                                   start=False, stop=False)
                    if p in (1, 2) and k // (2 * TH) == s:
                        c = (k % TH) * P
                        for w in (b, a):
                            eng.matmul(acc(s % 2, k // TH % 2, c, c + P), w[:, k, :], ident_r[:, :],
                                       start=False, stop=False)
                    summed = p == 0 and k not in added
                    if summed:
                        if k == first_summed and not (isinstance(G, int) and G == 0):
                            eng.wait_ge(csum_copied, 2 * G)
                        for h in range(2):
                            eng.matmul(csum(h), ones_r[:, :], hi[:, k % HI, h * BANK:(h + 1) * BANK],
                                       start=k == first_summed, stop=False)
                    eng.wait_ge(lo_ready, n + 1)
                    for h in range(2):
                        op = eng.matmul(acc(s % 2, h), a[:, k, :], lo[:, k % LO, h * BANK:(h + 1) * BANK],
                                        start=False, stop=last)
                    if summed:
                        for h in range(2):
                            op = eng.matmul(csum(h), ones_r[:, :], lo[:, k % LO, h * BANK:(h + 1) * BANK],
                                            start=False, stop=last)
                    if k == SUM_USED and added:
                        eng.wait_ge(piece_added, before + len(added))
                        for h in range(2):
                            op = eng.matmul(csum(h), ones_f[:, :], piece_sum[:, h * BANK:(h + 1) * BANK],
                                            start=False, stop=False)
                    op.then_inc(pieces_used, 1)
                run(bulk, steps)

            def turn(h, G, s):
                eng.wait_ge(acc_copied, 2 * G + h + 1)
                for q in range(TH):
                    op = eng.transpose(tail(h, q), cols[:, h, q, :], ident[:, :])
                op.then_inc(turned[h], 1)

            def turn_csum(h, G, s):
                eng.wait_ge(csum_copied, 2 * G + h + 1)
                eng.matmul(tail(h)[:, 0:TH], csum_rows[:, h, :], ident[:, 0:P:P // TH], start=True, stop=True)\
                   .then_inc(csum_turned[h], 1)

            def turn_message(h, G, s):
                eng.wait_ge(inv_step[h], 4 * G + 1)
                turn(h, G, s)

            def weigh(h, G, s):
                eng.wait_ge(acc_copied, 2 * G + h + 1)
                for q in range(TH):
                    op = eng.matmul(tail(h, q), cols[:, h, q, :], wl1[:, :], start=True, stop=True)
                op.then_inc(turned[h], 1)

            def turn_norm(h, G, s):
                eng.wait_ge(normed[h], norm_turn(G) + 1)
                for q in range(TH):
                    op = eng.transpose(tail(h, q), rows[:, h, q, :], ident[:, :])
                op.then_inc(norm_turned[h], 1)

            def second_weight(h, G, s):
                eng.wait_ge(norm_t_copied[h], G - SC + 1)
                for q in range(TH):
                    eng.matmul(tail(h, q), cols[:, h, q, :], wl2[:, :], start=True, stop=False)
                    eng.matmul(tail(h, q), ones_r[0:1, :], bl2_hi[:, :], start=False, stop=False)
                    op = eng.matmul(tail(h, q), ones_r[0:1, :], bl2_lo[:, :], start=False, stop=True)
                op.then_inc(hw_done[h], 1)

            def first_uv_weight(h, G, s):
                eng.wait_ge(norm_t_copied[h], G - SC + 1)
                for q in range(TH):
                    op = eng.matmul(tail(h, q), cols[:, h, q, :], mw[:, 0, :], start=True, stop=True)
                op.then_inc(hw_done[h], 1)

            def layer(i, kind):
                def step(h, G, s):
                    eng.wait_ge(act_ready[i - 1][h], mlp_turn(G) + 1)
                    eng.matmul(tail(h), mw[:, 3 * kind + i, :], rows[:, h, :, :].rearrange("p q f -> p (q f)"),
                               start=True, stop=True).then_inc(lin_done[i - 1][h], 1)
                return step

            def turn_v(h, G, s):
                eng.wait_ge(act_ready[2][h], mlp_turn(G) + 1)
                for q in range(TH):
                    op = eng.transpose(tail(h, q), rows[:, h, q, :], ident[:, :])
                op.then_inc(v_turned[h], 1)

            def weigh_v(kind):
                def step(h, G, s):
                    eng.wait_ge(act_ready[2][h], mlp_turn(G) + 1)
                    for q in range(TH):
                        op = eng.matmul(tail(h, q), rows[:, h, q, :], mw[:, 3 * kind, :], start=True, stop=True)
                    op.then_inc(v_turned[h], 1)
                return step

            def mlp(kind, turn_out):
                return lambda G, s: slots([(5, 7, layer(1, kind)), (11, 13, layer(2, kind)), (17, 19, turn_out)],
                                          G, s)

            def conv(first, second):
                return lambda G, s: slots([(2, 10, first), (11, 20, turn_norm), (15, 24, second)], G, s)

            def conv_end(first, second):
                return lambda G, s: slots([(2, 8, first), (11, 17, turn_norm), (15, 21, second)], G, s)

            message = lambda G, s: slots([(1, 2, turn_csum), (5, 11, turn_message)], G, s)
            uv, vu = mlp(0, weigh_v(1)), mlp(1, weigh_v(0))
            tails = {
                "start0": {}, "message": message, "message_end": message,
                "conv1": conv(weigh, second_weight), "conv1_end": conv_end(weigh, second_weight),
                "conv2": conv(turn, first_uv_weight), "conv2_end": conv_end(turn, first_uv_weight),
                "uv": uv, "uv_end": uv, "vu": vu, "vu_end": vu, "last": mlp(0, turn_v),
            }
            def weights_here():
                eng.wait_ge(w_landed, 16 * WEIGHT_LOADS)
                eng.wait_ge(bias_split, 2)

            nothing = dict.fromkeys(("message", "conv1", "conv2", "uv", "vu"), lambda base: {})
            whole_program(eng, superchunk, tails, nothing,
                          weights_here, lambda: None, unrolled=True)


_INS = ["x", "adj", "L1_gnn_weight", "L2_gnn_W", "L2_gnn_b"] + [
    f"L3_gnn_{d}_{n}{i}" for d in ("uv", "vu") for n in ("W", "b") for i in (1, 2, 3)]


def kernel(**inputs):
    import numpy as np
    import concourse.bacc as bacc
    from concourse.bass_utils import run_bass_kernel_spmd

    arrays = {name: np.ascontiguousarray(inputs[name]) for name in _INS}
    arrays["adj_t"] = np.ascontiguousarray(np.asarray(inputs["adj"]).T)
    arrays["L2_gnn_W"] = np.ascontiguousarray(np.asarray(inputs["L2_gnn_W"]).T)

    nc = bacc.Bacc("TRN2", target_bir_lowering=False, num_devices=1)
    ap = {name: nc.dram_tensor(f"in_{name}", a.shape, mybir.dt.from_np(a.dtype), kind="ExternalInput").ap()
          for name, a in arrays.items()}
    out = nc.dram_tensor("out_0", (N, P), F32, kind="ExternalOutput").ap()
    build(nc, ap["x"], ap["adj"], ap["adj_t"], ap["L1_gnn_weight"], ap["L2_gnn_W"], ap["L2_gnn_b"],
          [ap[f"L3_gnn_{d}_W{i}"] for d in ("uv", "vu") for i in (1, 2, 3)],
          [ap[f"L3_gnn_{d}_b{i}"] for d in ("uv", "vu") for i in (1, 2, 3)], out)
    result = run_bass_kernel_spmd(nc, [{f"in_{name}": a for name, a in arrays.items()}], core_ids=[0])
    return result.results[0]["out_0"]
```
